# Optimizing a Trainium2 kernel written in Bass

```python
import numpy as np
import jax
import jax.numpy as jnp

def _softmax(x, axis=-1):
    return jax.nn.softmax(x, axis=axis)

def _gelu(x):
    return jax.nn.gelu(x, approximate=True)

def _silu(x):
    return jax.nn.silu(x)

def _sigmoid(x):
    return jax.nn.sigmoid(x)

def _layernorm(x, axis=-1, eps=1e-05):
    m = jnp.mean(x, axis=axis, keepdims=True)
    v = jnp.var(x, axis=axis, keepdims=True)
    return (x - m) / jnp.sqrt(v + eps)

def _scatter_add(tgt, idx, src, axis=0):
    return tgt.at[idx].add(src)

def _segment_sum(src, seg, n):
    return jax.ops.segment_sum(src, seg, n)
kernel_name = 'mk_flamingo_gated_d1_seqx_r4_3c61ae'

def setup_inputs(seed: int=0):
    np.random.seed(seed)
    _w = jnp.asarray

    def _rec_inputs():
        import jax
        import jax.numpy as jnp
        _rk = jax.random.key(seed)
        x = -0.000125 + 0.9999 * jax.random.normal(jax.random.fold_in(_rk, 1), (4, 512, 512), jnp.float32)
        _lenS = 512 - jax.random.randint(jax.random.fold_in(_rk, 7), (4,), 0, max(1, 512 // 4) + 1, jnp.int32)
        _lenS2 = 512 - jax.random.randint(jax.random.fold_in(_rk, 8), (4,), 0, max(1, 512 // 4) + 1, jnp.int32)
        fside_BxS2xS2_0 = -3.05549e-07 + 0.0199987 * jax.random.normal(jax.random.fold_in(_rk, 11), (4, 512, 512), jnp.float32)
        _ctx_1024P = jax.random.normal(jax.random.fold_in(_rk, 12), (4, 16, 256), jnp.float32)
        _ctx_1024c = jax.random.dirichlet(jax.random.fold_in(_rk, 512), 0.3 * jnp.ones((16,), jnp.float32), (4, 512))
        _ctx_1024t = jnp.einsum('bsk,bkd->bsd', _ctx_1024c, _ctx_1024P)
        _ctx_1024t = _ctx_1024t * jax.lax.rsqrt(jnp.mean(jnp.square(_ctx_1024t)) + 1e-12) * 0.953939
        ctx_1024 = 6.82029e-06 + 0.0200006 * (_ctx_1024t + 0.3 * jax.random.normal(jax.random.fold_in(_rk, 612), (4, 512, 256), jnp.float32))
        _g = jax.random.normal(jax.random.fold_in(_rk, 9001), (2, 1), jnp.float32)
        _g = jnp.sign(_g) * jnp.maximum(jnp.abs(_g), 1.0) + (_g == 0) * 1.0
        g_xattn = _g[0]
        g_ffn = _g[1]
        return (x, fside_BxS2xS2_0, ctx_1024, g_xattn, g_ffn)
    x, fside_BxS2xS2_0, ctx_1024, g_xattn, g_ffn = _rec_inputs()

    def _L0_xattn_setup():
        import jax, jax.numpy as jnp
        import numpy as np
        EPS = 1e-06
        QMAX = 127.0

        def _smooth_quant_linear(x, w):
            amax_x = jnp.max(jnp.abs(x), axis=0)
            amax_w = jnp.max(jnp.abs(w), axis=0)
            s = jnp.sqrt(jnp.maximum(amax_x, EPS) / jnp.maximum(amax_w, EPS))
            s = jnp.maximum(s, EPS)
            xs = x / s
            ws = w * s
            x_scale = jnp.maximum(jnp.max(jnp.abs(xs), axis=-1, keepdims=True), EPS) / QMAX
            w_scale = jnp.maximum(jnp.max(jnp.abs(ws), axis=-1, keepdims=True), EPS) / QMAX
            x_q = jnp.clip(jnp.round(xs / x_scale), -QMAX, QMAX)
            w_q = jnp.clip(jnp.round(ws / w_scale), -QMAX, QMAX)
            return x_q @ w_q.T * x_scale * w_scale.T

        def _expert_forward(xe, guw, dw):
            h = _smooth_quant_linear(xe, guw)
            gate, up = jnp.split(h, 2, axis=-1)
            a = jax.nn.silu(gate) * up
            return _smooth_quant_linear(a, dw)
        key = jax.random.key(seed)
        k1, k2, k3 = jax.random.split(key, 3)
        E, T, D, I = (8, 512, 512, 256)
        x = jax.random.normal(k1, (E, T, D), dtype=jnp.float32)
        gate_up_weight = jax.random.normal(k2, (E, 2 * I, D), dtype=jnp.float32) * 0.02
        down_weight = jax.random.normal(k3, (E, D, I), dtype=jnp.float32) * 0.02
        return {'x': x, 'gate_up_weight': gate_up_weight, 'down_weight': down_weight}
    _L0_xattn_all = _L0_xattn_setup()
    _L0_xattn_in = {k: v for k, v in _L0_xattn_all.items() if k in ()}
    del _L0_xattn_all

    def _L0_ffn_setup():
        import jax, jax.numpy as jnp
        import numpy as np
        TOP_K = 2
        key = jax.random.key(seed)
        ks = jax.random.split(key, 5)
        B, T, D, E, H = (4, 512, 512, 8, 352)
        s = 1.0 / np.sqrt(D)
        sh = 1.0 / np.sqrt(H)
        return {'x': jax.random.normal(ks[0], (B, T, D), dtype=jnp.float32), 'Wg': jax.random.normal(ks[1], (E, D), dtype=jnp.float32) * s, 'W1': jax.random.normal(ks[2], (E, H, D), dtype=jnp.float32) * s, 'W2': jax.random.normal(ks[3], (E, H, D), dtype=jnp.float32) * s, 'W3': jax.random.normal(ks[4], (E, D, H), dtype=jnp.float32) * sh}
    _L0_ffn_all = _L0_ffn_setup()
    _L0_ffn_in = {k: v for k, v in _L0_ffn_all.items() if k in ('Wg', 'W1', 'W2', 'W3')}
    del _L0_ffn_all
    return {'x': x, 'fside_BxS2xS2_0': fside_BxS2xS2_0, 'ctx_1024': ctx_1024, 'g_xattn': g_xattn, 'g_ffn': g_ffn, 'L0_ffn_Wg': _L0_ffn_in['Wg'], 'L0_ffn_W1': _L0_ffn_in['W1'], 'L0_ffn_W2': _L0_ffn_in['W2'], 'L0_ffn_W3': _L0_ffn_in['W3']}

def reference(x, fside_BxS2xS2_0, ctx_1024, g_xattn, g_ffn, L0_ffn_Wg, L0_ffn_W1, L0_ffn_W2, L0_ffn_W3):
    import jax
    import jax.numpy as jnp

    def _L0_xattn_ref(x, gate_up_weight, down_weight):
        import jax, jax.numpy as jnp
        import numpy as np
        EPS = 1e-06
        QMAX = 127.0

        def _smooth_quant_linear(x, w):
            amax_x = jnp.max(jnp.abs(x), axis=0)
            amax_w = jnp.max(jnp.abs(w), axis=0)
            s = jnp.sqrt(jnp.maximum(amax_x, EPS) / jnp.maximum(amax_w, EPS))
            s = jnp.maximum(s, EPS)
            xs = x / s
            ws = w * s
            x_scale = jnp.maximum(jnp.max(jnp.abs(xs), axis=-1, keepdims=True), EPS) / QMAX
            w_scale = jnp.maximum(jnp.max(jnp.abs(ws), axis=-1, keepdims=True), EPS) / QMAX
            x_q = jnp.clip(jnp.round(xs / x_scale), -QMAX, QMAX)
            w_q = jnp.clip(jnp.round(ws / w_scale), -QMAX, QMAX)
            return x_q @ w_q.T * x_scale * w_scale.T

        def _expert_forward(xe, guw, dw):
            h = _smooth_quant_linear(xe, guw)
            gate, up = jnp.split(h, 2, axis=-1)
            a = jax.nn.silu(gate) * up
            return _smooth_quant_linear(a, dw)
        return jax.vmap(_expert_forward)(x, gate_up_weight, down_weight)

    def _L0_ffn_ref(x, Wg, W1, W2, W3):
        import jax, jax.numpy as jnp
        import numpy as np
        TOP_K = 2
        E = Wg.shape[0]
        scores = jnp.einsum('btd,ed->bte', x, Wg)
        topk_s, topk_i = jax.lax.top_k(scores, TOP_K)
        probs = jax.nn.softmax(topk_s, axis=-1)
        onehot = (topk_i[..., None] == jnp.arange(E)).astype(x.dtype)
        w = jnp.einsum('btk,btke->bte', probs, onehot)
        y = jnp.zeros_like(x)
        for e in range(E):
            h = jax.nn.silu(jnp.einsum('btd,hd->bth', x, W1[e])) * jnp.einsum('btd,hd->bth', x, W2[e])
            y = y + w[..., e:e + 1] * jnp.einsum('bth,dh->btd', h, W3[e])
        return y
    x = x + jnp.tanh(g_xattn[0]) * _L0_xattn_ref(_layernorm(x, axis=-1), fside_BxS2xS2_0, ctx_1024)
    x = x + jnp.tanh(g_ffn[0]) * _L0_ffn_ref(_layernorm(x, axis=-1), L0_ffn_Wg, L0_ffn_W1, L0_ffn_W2, L0_ffn_W3)
    return x

_drawn_inputs = setup_inputs


def setup_inputs(seed=0):
    import zlib

    import numpy as np

    out = dict(_drawn_inputs(seed))
    spreads = {}
    factors = {}
    for name, (base, spread) in spreads.items():
        noise = np.random.default_rng([zlib.crc32(name.encode()), seed]).standard_normal(out[name].shape)
        drawn = base * np.exp(spread * noise) if base else spread * noise
        out[name] = jnp.asarray(drawn.astype(out[name].dtype))
    for name, factor in factors.items():
        out[name] = (out[name] * factor).astype(out[name].dtype)
    return out
```

```python
from contextlib import ExitStack

import concourse.bass as bass
from concourse import mybir

F32 = mybir.dt.float32
F16 = mybir.dt.float16
BF16 = mybir.dt.bfloat16
I32 = mybir.dt.int32
U32 = mybir.dt.uint32
ALU = mybir.AluOpType
ACT = mybir.ActivationFunctionType
X = mybir.AxisListType.X

P = 128
B, S, D = 4, 512, 512
I = 256
T = S // P
KD = D // P
KI = I // P
E, H, TOPK = 8, 352, 2
KH = -(-H // P)
HP = KH * P
NTOK = B * T
ROWS = B * S
NT = (TOPK * ROWS - E) // P + E
TRASH = ROWS
WU = KD * 2 * H
WE = WU + KH * D
NB = 12
NA = 15
XV = 2
N_CONST = 13
LATE = 3
EARLY = E - LATE

EPS_LN = 1e-5
EPS = 1e-6
QMAX = 127.0
ROUND = 1.5 * 2.0 ** 23
WSCALE = 256.0
BIG = 3.0e38


def build_program(nc, x, w, wT, c, cT, g_x, g_f, wg, wexp, rows, xn2_rows):
    with ExitStack() as ctx:
        def sb(name, shape, dt):
            return ctx.enter_context(nc.sbuf_tensor(name, shape, dt))

        def bank(name):
            return ctx.enter_context(nc.psum_tensor(name, [P, 512], F32))

        def sem(name):
            return ctx.enter_context(nc.semaphore(name))

        w_hi = sb("w_hi", [P, E, WE], F16)
        w_lo = sb("w_lo", [P, E, WE], F16)
        w_stage = [sb("w_stage0", [P, WU], F32), sb("w_stage1", [P, WE - WU], F32)]

        hi_space = w_hi[:, EARLY:E, :].rearrange("p e n -> p (e n)").bitcast(F32)
        lo_space = w_lo[:, EARLY:E, :].rearrange("p e n -> p (e n)").bitcast(F32)
        n = T * D
        w_in = hi_space[:, 0:n].rearrange("p (t d) -> p t d", t=T)
        wT_in = hi_space[:, n:2 * n].rearrange("p (t d) -> p t d", t=KD)
        x_res = hi_space[:, 2 * n:3 * n].rearrange("p (t d) -> p t d", t=T)
        xn2 = lo_space[:, 0:n].rearrange("p (t d) -> p t d", t=T)
        xn2T = lo_space[:, n:2 * n].rearrange("p (t k m) -> p t k m", t=T, k=KD)
        c_in = lo_space[:, 2 * n:2 * n + T * I].rearrange("p (t d) -> p t d", t=T)
        cT_in = lo_space[:, 2 * n + T * I:2 * n + 2 * T * I].rearrange("p (k o) -> p k o", k=KI)

        x_in = sb("x_in", [P, T, D], F32)
        xn = sb("xn", [P, T, D], F32)
        xqT = sb("xqT", [P, KD, S], BF16)
        wqT = sb("wqT", [P, KD, D], BF16)
        inv_bc = sb("inv_bc", [P, D], F32)
        s_bc = sb("s_bc", [P, D], F32)
        wsc_bc = sb("wsc_bc", [P, D], F32)
        h_buf = sb("h_buf", [P, 2, 2 * I], F32)
        silu_g = [hi_space[:, 3 * n:3 * n + I], lo_space[:, 3 * n:3 * n + I]]
        a = sb("a", [P, T, I], F32)
        aqT = sb("aqT", [P, KI, S], BF16)
        cqT = sb("cqT", [P, KI, D], BF16)
        is2_bc = sb("is2_bc", [P, 2, I], F32)
        csc_bc = sb("csc_bc", [P, D], F32)
        y_tmp = sb("y_tmp", [P, 2, D], F32)

        logits = y_tmp[0:E, 1, :]

        def small(name, *shape):
            return sb(name, [P, *shape], F32)

        x_st, x_mv, x_var, x_rstd = small("x_st", T, 6), small("x_mv", T, 2), small("x_var", T), small("x_rstd", T)
        r_st, r_mv, r_var, r_rstd = small("r_st", T, 6), small("r_mv", T, 2), small("r_var", T), small("r_rstd", T)
        aw, aw_c, aw_r, ax = small("aw", KD), small("aw_c", KD), small("aw_r", KD), small("ax", KD)
        ratio, s_raw, s_col, s_inv = small("ratio", KD), small("s_raw", KD), small("s_col", KD), small("s_inv", KD)
        xs_max, x_sc, x_rq = small("xs_max", T), small("x_sc", T), small("x_rq", T)
        ws_max, w_sc, w_rq = small("ws_max", T), small("w_sc", T), small("w_rq", T)
        ac, ac_c, ac_r, aa = small("ac", KI), small("ac_c", KI), small("ac_r", KI), small("aa", KI)
        ratio2, s2_raw, s2_col, s2_inv = small("ratio2", KI), small("s2_raw", KI), small("s2_col", KI), small("s2_inv", KI)
        as_max, a_sc, a_rq = small("as_max", T), small("a_sc", T), small("a_rq", T)
        cs_max, c_sc, c_rq = small("cs_max", T), small("c_sc", T), small("c_rq", T)
        half, minus_half, round_col = small("half", T), small("minus_half", T), small("round_col", 1)
        gates, gates_t, spare = small("gates", 2), small("gates_t", 2), small("spare", 1)
        wgT = small("wgT", KD, E)
        ident = small("ident", P)

        scores = small("scores", NTOK, E)
        a_flat = a[:, :, :].rearrange("p t i -> p (t i)")
        ne = NTOK * E
        pref = small("pref", E)
        ohs = a_flat[:, 0:TOPK * ne].rearrange("p (k i e) -> p k i e", k=TOPK, e=E)
        tmp_e, sc2, pos_e = (a_flat[:, (TOPK + i) * ne:(TOPK + i + 1) * ne].rearrange("p (i e) -> p i e", e=E) for i in range(3))
        late_t = a_flat[:, (TOPK + 3) * ne:(TOPK + 3) * ne + NT * E].rearrange("p (t e) -> p t e", e=E)
        h_flat = h_buf[:, :, :].rearrange("p a i -> p (a i)")

        def pair(i):
            return h_flat[:, i * TOPK * NTOK:(i + 1) * TOPK * NTOK].rearrange("p (k i) -> p k i", k=TOPK)

        top, pick, prob, pos, tile_of, slot_of, tile_x = (pair(i) for i in range(7))
        gap, ex, den = pair(7)[:, 0, :], pair(7)[:, 1, :], pair(8)[:, 0, :]
        val = h_flat[:, 9 * TOPK * NTOK:12 * TOPK * NTOK].rearrange("p (v k i) -> p v k i", v=3, k=TOPK)
        at = 12 * TOPK * NTOK
        tab = h_flat[:, at:at + 3 * NT].rearrange("p (v t) -> p v t", v=3)
        te_f = h_flat[:, at + 3 * NT:at + 4 * NT]
        unf = h_flat[:, at + 4 * NT:at + 5 * NT]
        used = sb("used", [P, NTOK + 1, E], BF16)
        before = sb("before", [P, P], BF16)
        ones = sb("ones", [P, P], BF16)
        n_tiles, n_ends, n_starts, ones_e = small("n_tiles", E), small("n_ends", E), small("n_starts", E), small("ones_e", E)
        p_hi = sb("p_hi", [P, TOPK, NTOK], F16)
        iota_p = small("iota_p", P)
        iota_t = small("iota_t", NT)
        row_id = small("row_id", NTOK)
        trash_id = small("trash_id", 1)
        te = sb("te", [P, NT], I32)
        gather_id = y_tmp[:, 0, NT:2 * NT].bitcast(U32)
        add_id = y_tmp[:, 0, 2 * NT:3 * NT].bitcast(U32)
        slot_w = y_tmp[:, 0, 0:NT]
        zeros = x_in[:, 0, :]
        in_slot = x_in[:, :, :].rearrange("p t d -> p (t d)").bitcast(F16)[:, 0:TOPK * NTOK * P].rearrange("p (j m) -> p j m", m=P)
        entry = xn[:, :, :].rearrange("p t d -> p (t d)").bitcast(F16)[:, 0:TOPK * NTOK * 3 * NT].rearrange(
            "p (j v t) -> p j v t", v=3, t=NT)
        in_tile = wqT[:, :, :].rearrange("p t d -> p (t d)").bitcast(F16)[:, 0:TOPK * NTOK * NT].rearrange(
            "p (j t) -> p j t", t=NT)

        XG = 3
        xg = xn[:, 0:XG, :]
        y_out = x_in[:, 0:XG, :]
        x_hi = inv_bc[:, :].bitcast(F16)[:, 0:D].rearrange("p (k m) -> p k m", k=KD)
        x_lo = inv_bc[:, :].bitcast(F16)[:, D:2 * D].rearrange("p (k m) -> p k m", k=KD)
        gate_s = wsc_bc[:, 0:H]
        h = csc_bc[:, 0:HP]
        h_hi = s_bc[:, :].bitcast(F16)[:, 0:HP].rearrange("p (k m) -> p k m", k=KH)
        h_lo = s_bc[:, :].bitcast(F16)[:, HP:2 * HP].rearrange("p (k m) -> p k m", k=KH)
        AHEAD = XG + 2
        turn_ix = sb("turn_ix", [P, XG, 2], U32)
        turn_id = y_tmp[:, 0, NT + AHEAD:3 * NT - AHEAD].rearrange("p (v t) -> p v t", v=2).bitcast(U32)

        pA = [bank("pA0"), bank("pA1")]
        pB = [bank("pB0"), bank("pB1")]
        pH = [bank("pH0"), bank("pH1")]
        pY = [bank("pY0"), bank("pY1")]

        def h_bank(t):
            return pH[t] if t < 2 else pA[3 - t]

        names = """consts_a consts_v consts_m x_in_s w_in_s wT_in_s c_in_s cT_in_s res_in_s g_in_s wg_in_s zero_s
            x_stats x_aggr x_var_s x_rstd_s xn_s aw_s awc_s awr_s ax_s ratio_s sraw_s scol_s sinv_s xsv_s
            invbc_s sbc_s xs_s ws_s xsmax_s xsc_s xrq_s wsmax_s wsc_s wrq_s xq_s wq_s
            tA tA_v tA_a wqT_s xqT_s wscbc_s mm1 h_s silu_s a_s
            ac_s acc_s acr_s aa_s ratio2_s s2raw_s s2col_s s2inv_s is2_s as_s cs_s asmax_s asc_s arq_s
            csmax_s csc_s crq_s aq_s cq_s tB tB_v tB_a cqT_s aqT_s cscbc_s mm2 y_s res_s
            r_stats r_aggr r_var_s r_rstd_s xn2_s xn2T_s logits logits_s router score_s x_out_s xn2_out_s gate_t_s
            wl0 wl1 whi_s wlo_s
            rt exp_s used_s prefix table idx_s te_s table_free
            h_pad_s ix_s gather0 gather1 gather2 pXt x_hi_s x_lo_s up gate_s_s h_ready pTt h_hi_s h_lo_s down y_ready add0 add1 add2 init_s"""
        s = {k: sem(k) for k in names.split()}
        wl = [s["wl0"], s["wl1"]]
        gathered = [s["gather0"], s["gather1"], s["gather2"]]
        added = [s["add0"], s["add1"], s["add2"]]

        def wait(eng, name, count):
            if not (isinstance(count, int) and count <= 0):
                eng.wait_ge(s[name] if isinstance(name, str) else name, count)

        PIECES = [(0, WU), (WU, WE)]

        def piece(half, e, n):
            return half[:, bass.ds(e, 1), PIECES[n][0]:PIECES[n][1]].rearrange("p a n -> p (a n)")

        block = ctx.enter_context(nc.Block())

        @block.sync
        def _(sp):
            def load_w(e):
                for n, (lo, hi) in enumerate(PIECES):
                    wait(sp, "wlo_s", 2 * (e - 1) + n + 1)

                    sp.dma_start(w_stage[n][:, :], wexp[bass.ds(e, 1), :, lo:hi].rearrange("a p n -> p (a n)")
                                 ).then_inc(wl[n], 16)

            def batch(dram, b):
                return dram[bass.ds(b, 1), :, :, :].rearrange("a p t d -> p (a t) d")

            def load_x(b):
                wait(sp, "xn_s", T * b)
                sp.dma_start(x_in[:, :, :], batch(x, b)).then_inc(s["x_in_s"], 16)
                wait(sp, "aw_s", b)
                sp.dma_start(wT_in, batch(wT, b)).then_inc(s["wT_in_s"], 16)

            def load_first(b):
                wait(sp, "wqT_s", KD * b)
                sp.dma_start(w_in, batch(w, b)).then_inc(s["w_in_s"], 16)

            def load_cT(b):
                wait(sp, "ac_s", b)
                sp.dma_start(cT_in, batch(cT, b)).then_inc(s["cT_in_s"], 16)

            def load_c(b):
                wait(sp, "cqT_s", KI * b)
                sp.dma_start(c_in, batch(c, b)).then_inc(s["c_in_s"], 16)

            def load_residual(b):
                wait(sp, "x_out_s", 16 * b)
                wait(sp, "xn2_s", T * b)
                sp.dma_start(x_res, batch(x, b)).then_inc(s["res_in_s"], 16)

            load_x(0)
            load_first(0)
            sp.dma_start(gates[:, 0:1], g_x.to_broadcast([P, 1])).then_inc(s["g_in_s"], 16)
            sp.dma_start(gates[:, 1:2], g_f.to_broadcast([P, 1])).then_inc(s["g_in_s"], 16)
            sp.dma_start(wgT[:, :, :], wg).then_inc(s["wg_in_s"], 16)
            load_w(0)
            load_x(1)
            load_cT(0)
            load_c(0)
            load_residual(0)
            load_w(1)
            load_first(1)
            load_w(2)
            for b in range(1, B):
                if b + 1 < B:
                    load_x(b + 1)
                load_cT(b)
                if b + 2 < EARLY:
                    load_w(b + 2)
                load_c(b)
                if b + 1 < B:
                    load_first(b + 1)
                load_residual(b)
            wait(sp, "xn_s", T * B)
            wait(sp, "zero_s", 1)
            sp.dma_start(rows[TRASH:TRASH + P, :], zeros).then_inc(s["init_s"], 16)
            for e in range(EARLY, E):
                load_w(e)
            sp.wait_ge(s["x_out_s"], 16 * B)
            sp.wait_ge(s["xn2_out_s"], 16 * B)
            sp.wait_ge(s["init_s"], 16)
            for j in range(XG):
                sp.wait_ge(added[j], 16 * len(range(j, NT, XG)))

        @block.gpsimd
        def _(g):
            g.memset(ident[:, :], 0.0).then_inc(s["consts_m"], 1)
            g.memset(before[:, :], 1.0).then_inc(s["consts_m"], 1)
            g.memset(ones[:, :], 1.0).then_inc(s["consts_a"], 1)
            g.memset(half[:, :], 0.5).then_inc(s["consts_a"], 1)
            g.memset(minus_half[:, :], -0.5).then_inc(s["consts_a"], 1)
            g.memset(round_col[:, :], ROUND).then_inc(s["consts_a"], 1)
            g.memset(ones_e[:, :], 1.0).then_inc(s["consts_a"], 1)
            g.memset(used[:, NTOK, :], 0.0).then_inc(s["consts_a"], 1)
            g.wait_ge(s["consts_m"], 2)
            g.affine_select(out=ident[:, :], in_=ident[:, :], compare_op=ALU.not_equal, fill=1.0, base=0,
                            pattern=[[-1, P]], channel_multiplier=1).then_inc(s["consts_a"], 1)
            g.affine_select(out=before[:, :], in_=before[:, :], compare_op=ALU.is_gt, fill=0.0, base=0,
                            pattern=[[1, P]], channel_multiplier=-1).then_inc(s["consts_a"], 1)
            g.iota(pref[:, :], pattern=[[-1, E]], base=E, channel_multiplier=0,
                   allow_small_or_imprecise_dtypes=True).then_inc(s["consts_a"], 1)
            g.iota(iota_p[:, :], pattern=[[1, P]], base=0, channel_multiplier=0,
                   allow_small_or_imprecise_dtypes=True).then_inc(s["consts_a"], 1)
            g.iota(iota_t[:, :], pattern=[[1, NT]], base=0, channel_multiplier=0,
                   allow_small_or_imprecise_dtypes=True).then_inc(s["consts_a"], 1)
            g.iota(row_id[:, :], pattern=[[P, NTOK]], base=1, channel_multiplier=1,
                   allow_small_or_imprecise_dtypes=True).then_inc(s["consts_a"], 1)
            g.iota(trash_id[:, :], pattern=[[0, 1]], base=TRASH + 1, channel_multiplier=1,
                   allow_small_or_imprecise_dtypes=True).then_inc(s["consts_a"], 1)
            g.wait_ge(s["consts_a"], N_CONST)

            def first_rstd(b):
                wait(g, "x_var_s", b + 1)
                g.tensor_tensor(x_rstd[:, :], x_var[:, :], minus_half[:, :], ALU.pow).then_inc(s["x_rstd_s"], 1)

            def first_root(b):
                wait(g, "ratio_s", b + 1)
                g.tensor_tensor(s_raw[:, :], ratio[:, :], half[:, 0:KD], ALU.pow).then_inc(s["sraw_s"], 1)

            def first_scale_x(b):
                wait(g, "invbc_s", b + 1)
                wait(g, "ax_s", KD * (b + 1))
                for t in range(XV, T):
                    g.tensor_tensor(xn[:, t, :], xn[:, t, :], inv_bc[:, :], ALU.mult).then_inc(s["xs_s"], 1)

            def first_scale_w(b):
                wait(g, "sbc_s", b + 1)
                wait(g, "w_in_s", 16 * (b + 1))
                for t in range(T):
                    g.tensor_tensor(w_in[:, t, :], w_in[:, t, :], s_bc[:, :], ALU.mult).then_inc(s["ws_s"], 1)

            def second_root(b):
                wait(g, "ratio2_s", b + 1)
                g.tensor_tensor(s2_raw[:, :], ratio2[:, :], half[:, 0:KI], ALU.pow).then_inc(s["s2raw_s"], 1)

            def second_scale(b):
                wait(g, "is2_s", b + 1)
                wait(g, "aa_s", KI * (b + 1))
                for t in range(T):
                    g.tensor_tensor(a[:, t, :], a[:, t, :], is2_bc[:, 0, :], ALU.mult).then_inc(s["as_s"], 1)

            def second_scale_c(b):
                wait(g, "c_in_s", 16 * (b + 1))
                for t in range(T):
                    g.tensor_tensor(c_in[:, t, :], c_in[:, t, :], is2_bc[:, 1, :], ALU.mult).then_inc(s["cs_s"], 1)

            def residual(b):
                wait(g, "res_in_s", 16 * (b + 1))
                for t in range(T):
                    wait(g, "y_s", T * b + t + 1)
                    g.tensor_tensor(x_res[:, t, :], x_res[:, t, :], y_tmp[:, t % 2, :], ALU.add).then_inc(s["res_s"], 1)

            def second_rstd(b):
                wait(g, "r_var_s", b + 1)
                g.tensor_tensor(r_rstd[:, :], r_var[:, :], minus_half[:, :], ALU.pow).then_inc(s["r_rstd_s"], 1)

            def both(b, more=True):
                second_scale(b - 1)
                first_scale_x(b)
                second_scale_c(b - 1)
                first_scale_w(b)
                residual(b - 1)
                if more:
                    first_rstd(b + 1)
                second_rstd(b - 1)
                second_root(b)
                if more:
                    first_root(b + 1)

            first_rstd(0)
            first_root(0)
            first_scale_x(0)
            first_scale_w(0)
            first_rstd(1)
            second_root(0)
            first_root(1)
            with g.Fori(1, B - 1) as b:
                both(b)
            both(B - 1, more=False)
            second_scale(B - 1)
            second_scale_c(B - 1)
            residual(B - 1)
            second_rstd(B - 1)

            g.wait_ge(s["idx_s"], 3)
            g.wait_ge(s["xn2_out_s"], 16 * B)
            g.wait_ge(s["x_out_s"], 16 * B)
            g.wait_ge(s["init_s"], 16)

            def gather(j, ids):
                g.indirect_dma_start(out=xg[:, j, :], out_offset=None, in_=xn2_rows,
                                     in_offset=bass.IndirectOffsetOnAxis(ap=ids, axis=0)).then_inc(gathered[j], 16)

            def add_rows(j, ids):
                g.indirect_dma_start(out=rows, out_offset=bass.IndirectOffsetOnAxis(ap=ids, axis=0),
                                     in_=y_out[:, j, :], in_offset=None, compute_op=ALU.add).then_inc(added[j], 16)

            def ids_of(t, j):
                g.tensor_copy(turn_ix[:, j, :].rearrange("p (v a) -> p v a", a=1), turn_id[:, :, bass.ds(t, 1)]
                              ).then_inc(s["ix_s"], 1)

            for t in range(AHEAD):
                if t >= XG:
                    g.wait_ge(s["pXt"], t - XG + 1)
                gather(t % XG, gather_id[:, t:t + 1])
                if t == XG - 1:
                    ids_of(0, 0)
            turns = (NT - AHEAD) // XG
            with g.Fori(0, turns) as i:
                for j in range(XG):
                    t = i * XG + j
                    g.wait_ge(s["ix_s"], t + 1)
                    g.wait_ge(s["y_ready"], t + 1)
                    g.wait_ge(gathered[j], (i + 2) * 16)
                    g.wait_ge(added[(j - 1) % XG], (i + (1 if j else 0)) * 16)
                    ids_of(t + 1, (j + 1) % XG)
                    add_rows(j, turn_ix[:, j, 1:2])
                    gather((j + AHEAD) % XG, turn_ix[:, j, 0:1])
            for t in range(turns * XG, NT):
                g.wait_ge(s["y_ready"], t + 1)
                g.wait_ge(added[(t - 1) % XG], ((t - 1) // XG + 1) * 16)
                add_rows(t % XG, add_id[:, t:t + 1])
                if t + AHEAD < NT:
                    gather((t + AHEAD) % XG, gather_id[:, t + AHEAD:t + AHEAD + 1])

        @block.vector
        def _(v):
            def split_low(e):
                for n, (lo, hi) in enumerate(PIECES):
                    wait(v, "whi_s", 2 * e + n + 1)
                    v.scalar_tensor_tensor(out=piece(w_lo, e, n), in0=w_stage[n][:, :], scalar=WSCALE,
                                           in1=piece(w_hi, e, n), op0=ALU.mult, op1=ALU.subtract).then_inc(s["wlo_s"], 1)

            def first_stats(b):
                wait(v, "x_in_s", 16 * (b + 1))
                for t in range(T):
                    v.bn_stats(x_st[:, t, :], x_in[:, t, :]).then_inc(s["x_stats"], 1)
                wait(v, "x_stats", T * (b + 1))
                v.memset(spare[:, :], 0.0)
                for t in range(T):
                    v.bn_aggr(x_mv[:, t, :], x_st[:, t, :]).then_inc(s["x_aggr"], 1)
                wait(v, "x_aggr", T * (b + 1))
                v.tensor_scalar(x_var[:, :], x_mv[:, :, 1], EPS_LN, None, ALU.add).then_inc(s["x_var_s"], 1)

            def first_weight_max(b):
                wait(v, "wT_in_s", 16 * (b + 1))
                v.tensor_reduce(aw[:, :], wT_in, X, ALU.max, apply_absolute_value=True).then_inc(s["aw_s"], 1)
                wait(v, "aw_s", b + 1)
                v.tensor_scalar(aw_c[:, :], aw[:, :], EPS, None, ALU.max).then_inc(s["awc_s"], 1)
                wait(v, "awc_s", b + 1)
                v.reciprocal(aw_r[:, :], aw_c[:, :]).then_inc(s["awr_s"], 1)

            def first_norm(b):
                wait(v, "x_rstd_s", b + 1)
                wait(v, "xqT_s", KD * b)
                for t in range(T):
                    v.tensor_scalar(xn[:, t, :], x_in[:, t, :], x_mv[:, t, 0:1], x_rstd[:, t:t + 1],
                                    ALU.subtract, ALU.mult).then_inc(s["xn_s"], 1)

            def first_col_max(b):
                for k in range(KD):
                    wait(v, "tA", NA * b + k + 1)
                    v.tensor_reduce(ax[:, k:k + 1], pA[k % 2][:, :], X, ALU.max,
                                    apply_absolute_value=True).then_inc(s["ax_s"], 1)

            def first_ratio(b):
                wait(v, "ax_s", KD * (b + 1))
                wait(v, "awr_s", b + 1)
                v.scalar_tensor_tensor(out=ratio[:, :], in0=ax[:, :], scalar=EPS, in1=aw_r[:, :],
                                       op0=ALU.max, op1=ALU.mult).then_inc(s["ratio_s"], 1)

            def first_smooth(b):
                wait(v, "sraw_s", b + 1)
                v.tensor_scalar(s_col[:, :], s_raw[:, :], EPS, None, ALU.max).then_inc(s["scol_s"], 1)
                wait(v, "scol_s", b + 1)
                v.reciprocal(s_inv[:, :], s_col[:, :]).then_inc(s["sinv_s"], 1)

            def first_scale_x(b):
                wait(v, "invbc_s", b + 1)
                for t in range(XV):
                    v.tensor_tensor(xn[:, t, :], xn[:, t, :], inv_bc[:, :], ALU.mult).then_inc(s["xsv_s"], 1)

            def first_row_scale(b):
                wait(v, "xsv_s", XV * (b + 1))
                wait(v, "xs_s", (T - XV) * (b + 1))
                v.tensor_reduce(xs_max[:, :], xn[:, :, :], X, ALU.max, apply_absolute_value=True).then_inc(s["xsmax_s"], 1)
                wait(v, "xsmax_s", b + 1)
                wait(v, "h_s", T * b)
                v.tensor_scalar(x_sc[:, :], xs_max[:, :], EPS, 1.0 / QMAX, ALU.max, ALU.mult).then_inc(s["xsc_s"], 1)
                wait(v, "xsc_s", b + 1)
                v.reciprocal(x_rq[:, :], x_sc[:, :]).then_inc(s["xrq_s"], 1)
                wait(v, "xrq_s", b + 1)
                for t in range(T):
                    v.tensor_scalar(xn[:, t, :], xn[:, t, :], x_rq[:, t:t + 1], ROUND, ALU.mult, ALU.add).then_inc(s["xq_s"], 1)

            def first_weight_scale(b):
                for t in range(0, T, 2):
                    wait(v, "ws_s", T * b + t + 2)
                    v.tensor_reduce(ws_max[:, t:t + 2], w_in[:, t:t + 2, :], X, ALU.max,
                                    apply_absolute_value=True).then_inc(s["wsmax_s"], 1)
                wait(v, "wsmax_s", T // 2 * (b + 1))
                v.tensor_scalar(w_sc[:, :], ws_max[:, :], EPS, 1.0 / QMAX, ALU.max, ALU.mult).then_inc(s["wsc_s"], 1)
                wait(v, "wsc_s", b + 1)
                v.reciprocal(w_rq[:, :], w_sc[:, :]).then_inc(s["wrq_s"], 1)

            def first_out(b):
                wait(v, "wscbc_s", b + 1)
                wait(v, "aqT_s", KI * b)
                for t in range(T + 1):
                    if t < T:
                        wait(v, "mm1", T * b + t + 1)
                        wait(v, "a_s", T * b + t - 1)
                        v.scalar_tensor_tensor(out=h_buf[:, t % 2, :], in0=h_bank(t)[:, :], scalar=x_sc[:, t:t + 1],
                                               in1=wsc_bc[:, :], op0=ALU.mult, op1=ALU.mult).then_inc(s["h_s"], 1)
                    if t > 0:
                        wait(v, "silu_s", T * b + t)
                        v.tensor_tensor(a[:, t - 1, :], silu_g[(t - 1) % 2], h_buf[:, (t - 1) % 2, I:2 * I],
                                        ALU.mult).then_inc(s["a_s"], 1)

            def second_weight_max(b):
                wait(v, "cT_in_s", 16 * (b + 1))
                v.tensor_reduce(ac[:, :], cT_in, X, ALU.max, apply_absolute_value=True).then_inc(s["ac_s"], 1)
                wait(v, "ac_s", b + 1)
                v.tensor_scalar(ac_c[:, :], ac[:, :], EPS, None, ALU.max).then_inc(s["acc_s"], 1)
                wait(v, "acc_s", b + 1)
                v.reciprocal(ac_r[:, :], ac_c[:, :]).then_inc(s["acr_s"], 1)

            def second_col_max(b):
                for k in range(KI):
                    wait(v, "tB", NB * b + k + 1)
                    v.tensor_reduce(aa[:, k:k + 1], pB[k % 2][:, :], X, ALU.max,
                                    apply_absolute_value=True).then_inc(s["aa_s"], 1)
                wait(v, "aa_s", KI * (b + 1))
                wait(v, "acr_s", b + 1)
                v.scalar_tensor_tensor(out=ratio2[:, :], in0=aa[:, :], scalar=EPS, in1=ac_r[:, :],
                                       op0=ALU.max, op1=ALU.mult).then_inc(s["ratio2_s"], 1)

            def second_smooth(b):
                wait(v, "s2raw_s", b + 1)
                v.tensor_scalar(s2_col[:, :], s2_raw[:, :], EPS, None, ALU.max).then_inc(s["s2col_s"], 1)
                wait(v, "s2col_s", b + 1)
                v.reciprocal(s2_inv[:, :], s2_col[:, :]).then_inc(s["s2inv_s"], 1)

            def second_a_scale(b):
                wait(v, "as_s", T * (b + 1))
                v.tensor_reduce(as_max[:, :], a[:, :, :], X, ALU.max, apply_absolute_value=True).then_inc(s["asmax_s"], 1)
                wait(v, "asmax_s", b + 1)
                v.tensor_scalar(a_sc[:, :], as_max[:, :], EPS, 1.0 / QMAX, ALU.max, ALU.mult).then_inc(s["asc_s"], 1)
                wait(v, "asc_s", b + 1)
                v.reciprocal(a_rq[:, :], a_sc[:, :]).then_inc(s["arq_s"], 1)
                wait(v, "arq_s", b + 1)
                for t in range(T):
                    v.tensor_scalar(a[:, t, :], a[:, t, :], a_rq[:, t:t + 1], ROUND, ALU.mult, ALU.add).then_inc(s["aq_s"], 1)

            def second_c_scale(b):
                wait(v, "cs_s", T * (b + 1))
                v.tensor_reduce(cs_max[:, :], c_in, X, ALU.max, apply_absolute_value=True).then_inc(s["csmax_s"], 1)
                wait(v, "csmax_s", b + 1)
                v.tensor_scalar(c_sc[:, :], cs_max[:, :], EPS, 1.0 / QMAX, ALU.max, ALU.mult).then_inc(s["csc_s"], 1)
                wait(v, "csc_s", b + 1)
                v.reciprocal(c_rq[:, :], c_sc[:, :]).then_inc(s["crq_s"], 1)

            def second_out(b):
                wait(v, "cscbc_s", b + 1)
                for t in range(T):
                    wait(v, "mm2", T * b + t + 1)
                    if t >= 2:
                        wait(v, "res_s", T * b + t - 1)
                    v.scalar_tensor_tensor(out=y_tmp[:, t % 2, :], in0=pY[t % 2][:, :], scalar=a_sc[:, t:t + 1],
                                           in1=csc_bc[:, :], op0=ALU.mult, op1=ALU.mult).then_inc(s["y_s"], 1)

            def second_norm(b):
                for t in range(T):
                    wait(v, "res_s", T * b + t + 1)
                    v.bn_stats(r_st[:, t, :], x_res[:, t, :]).then_inc(s["r_stats"], 1)
                wait(v, "r_stats", T * (b + 1))
                v.memset(spare[:, :], 0.0)
                for t in range(T):
                    v.bn_aggr(r_mv[:, t, :], r_st[:, t, :]).then_inc(s["r_aggr"], 1)
                wait(v, "r_aggr", T * (b + 1))
                v.tensor_scalar(r_var[:, :], r_mv[:, :, 1], EPS_LN, None, ALU.add).then_inc(s["r_var_s"], 1)

            def second_norm_out(b):
                wait(v, "r_rstd_s", b + 1)
                wait(v, "xn2_out_s", 16 * b)
                wait(v, "xn2T_s", T * b)
                for t in range(T):
                    v.tensor_scalar(xn2[:, t, :], x_res[:, t, :], r_mv[:, t, 0:1], r_rstd[:, t:t + 1],
                                    ALU.subtract, ALU.mult).then_inc(s["xn2_s"], 1)

            def second_scores(b):
                wait(v, "router", b + 1)
                v.tensor_copy(scores[:, bass.ds(b * T, T), :],
                              pY[1][:, 0:T * E].rearrange("p (t e) -> p t e", t=T)).then_inc(s["score_s"], 1)

            def both(b, more=True):
                first_scale_x(b)
                second_a_scale(b - 1)
                first_row_scale(b)
                second_c_scale(b - 1)
                split_low(b + 1)
                first_weight_scale(b)
                second_out(b - 1)
                if more:
                    first_stats(b + 1)
                second_norm(b - 1)
                if more:
                    first_norm(b + 1)
                second_norm_out(b - 1)
                second_weight_max(b)
                first_out(b)
                second_col_max(b)
                if more:
                    first_weight_max(b + 1)
                    first_col_max(b + 1)
                    first_ratio(b + 1)
                second_smooth(b)
                second_scores(b - 1)
                if more:
                    first_smooth(b + 1)

            first_stats(0)
            first_weight_max(0)
            first_norm(0)
            first_col_max(0)
            first_ratio(0)
            first_smooth(0)
            first_scale_x(0)
            first_row_scale(0)
            split_low(0)
            first_weight_scale(0)
            first_stats(1)
            first_norm(1)
            first_weight_max(1)
            second_weight_max(0)
            first_out(0)
            second_col_max(0)
            first_col_max(1)
            first_ratio(1)
            second_smooth(0)
            first_smooth(1)
            split_low(1)
            with v.Fori(1, B - 1) as b:
                both(b)
            both(B - 1, more=False)
            b = B - 1
            second_a_scale(b)
            second_c_scale(b)
            second_out(b)
            second_norm(b)
            v.memset(zeros, 0.0).then_inc(s["zero_s"], 1)
            second_norm_out(b)
            second_scores(b)

            v.wait_ge(s["cscbc_s"], B)
            v.memset(h[:, H:HP], 0.0).then_inc(s["h_pad_s"], 1)
            v.wait_ge(s["consts_a"], N_CONST)
            v.wait_ge(s["score_s"], B)
            n_rt = [0]

            def step(instruction):
                n_rt[0] += 1
                instruction.then_inc(s["rt"], 1)
                v.wait_ge(s["rt"], n_rt[0])

            def over_e(ap):
                return ap.rearrange("p (i a) -> p i a", a=1).to_broadcast([P, NTOK, E])

            pref_b = pref[:, :].rearrange("p (a e) -> p a e", a=1).to_broadcast([P, NTOK, E])
            for k in range(TOPK):
                src = scores if k == 0 else sc2
                step(v.tensor_reduce(top[:, k, :], src[:, :, :], X, ALU.max))
                step(v.tensor_tensor(tmp_e[:, :, :], src[:, :, :], over_e(top[:, k, :]), ALU.is_equal))
                step(v.tensor_tensor(tmp_e[:, :, :], tmp_e[:, :, :], pref_b, ALU.mult))
                step(v.tensor_reduce(pick[:, k, :], tmp_e[:, :, :], X, ALU.max))
                step(v.tensor_tensor(ohs[:, k, :, :], pref_b, over_e(pick[:, k, :]), ALU.is_equal))
                if k == 0:
                    step(v.scalar_tensor_tensor(out=sc2[:, :, :], in0=ohs[:, 0, :, :], scalar=-BIG, in1=scores[:, :, :],
                                                op0=ALU.mult, op1=ALU.add))
            v.tensor_tensor(used[:, 0:NTOK, :], ohs[:, 0, :, :], ohs[:, 1, :, :], ALU.add).then_inc(s["used_s"], 1)
            step(v.tensor_tensor(gap, top[:, 1, :], top[:, 0, :], ALU.subtract))
            gap_at = n_rt[0]
            v.wait_ge(s["prefix"], 1)
            step(v.tensor_scalar(n_tiles[:, :], pH[0][:, NTOK * E:(NTOK + 1) * E], 1.0 / P,
                                 (P - 1.0) / P - 0.5 + 1.0 / 512, ALU.mult, ALU.add))
            step(v.tensor_scalar(n_tiles[:, :], n_tiles[:, :], ROUND, ROUND, ALU.add, ALU.subtract))
            step(v.tensor_tensor_scan(n_ends[:, :], ones_e[:, :], n_tiles[:, :], 0.0, ALU.mult, ALU.add))
            step(v.tensor_tensor(n_starts[:, :], n_ends[:, :], n_tiles[:, :], ALU.subtract))
            starts_b = n_starts[:, :].rearrange("p (a e) -> p a e", a=1).to_broadcast([P, NTOK, E])
            step(v.scalar_tensor_tensor(out=pos_e[:, :, :], in0=starts_b, scalar=float(P),
                                        in1=pH[0][:, 0:NTOK * E].rearrange("p (i e) -> p i e", e=E),
                                        op0=ALU.mult, op1=ALU.add))
            for k in range(TOPK):
                step(v.tensor_tensor(tmp_e[:, :, :], ohs[:, k, :, :], pos_e[:, :, :], ALU.mult))
                step(v.tensor_reduce(pos[:, k, :], tmp_e[:, :, :], X, ALU.add))
            step(v.tensor_scalar(tile_x[:, :, :], pos[:, :, :], 1.0 / P, -0.5 + 1.0 / 512, ALU.mult, ALU.add))
            step(v.tensor_scalar(tile_of[:, :, :], tile_x[:, :, :], ROUND, ROUND, ALU.add, ALU.subtract))
            step(v.scalar_tensor_tensor(out=slot_of[:, :, :], in0=tile_of[:, :, :], scalar=-float(P), in1=pos[:, :, :],
                                        op0=ALU.mult, op1=ALU.add))
            v.wait_ge(s["exp_s"], 1)
            step(v.tensor_scalar(den, ex, 1.0, None, ALU.add))
            step(v.reciprocal(prob[:, 0, :], den))
            step(v.tensor_tensor(prob[:, 1, :], ex, prob[:, 0, :], ALU.mult))
            for k in range(TOPK):
                v.tensor_copy(val[:, 0, k, :], row_id[:, :])
            v.tensor_copy(p_hi[:, :, :], prob[:, :, :])
            step(v.tensor_copy(val[:, 1, :, :], prob[:, :, :]))
            step(v.tensor_tensor(val[:, 2, :, :], prob[:, :, :], p_hi[:, :, :], ALU.subtract))
            J = TOPK * NTOK
            tile_b = tile_of[:, :, :].rearrange("p k i -> p (k i)").rearrange("p (j a) -> p j a", a=1).to_broadcast([P, J, NT])
            iota_tb = iota_t[:, :].rearrange("p (a t) -> p a t", a=1).to_broadcast([P, J, NT])
            step(v.tensor_tensor(in_tile, iota_tb, tile_b, ALU.is_equal))
            for n_v in range(3):
                src = p_hi[:, :, :] if n_v == 1 else val[:, n_v, :, :]
                val_b = src.rearrange("p k i -> p (k i)").rearrange("p (j a) -> p j a", a=1).to_broadcast([P, J, NT])
                ins = v.tensor_tensor(entry[:, :, n_v, :], in_tile, val_b, ALU.mult)
            slot_b = slot_of[:, :, :].rearrange("p k i -> p (k i)").rearrange("p (j a) -> p j a", a=1).to_broadcast([P, J, P])
            iota_pb = iota_p[:, :].rearrange("p (a m) -> p a m", a=1).to_broadcast([P, J, P])
            v.wait_ge(s["init_s"], 16)
            v.tensor_tensor(in_slot, iota_pb, slot_b, ALU.is_equal).then_inc(s["table_free"], 1)
            ends_b = n_ends[:, :].rearrange("p (a e) -> p a e", a=1).to_broadcast([P, NT, E])
            iota_te = iota_t[:, :].rearrange("p (t a) -> p t a", a=1).to_broadcast([P, NT, E])
            step(v.tensor_tensor(late_t[:, :, :], iota_te, ends_b, ALU.is_ge))
            step(v.tensor_reduce(te_f[:, :], late_t[:, :, :], X, ALU.add))
            v.tensor_scalar(te[:, :], te_f[:, :], float(E - 1), None, ALU.min).then_inc(s["te_s"], 1)
            v.wait_ge(s["table"], 1)
            step(v.tensor_copy(tab[:, :, :], pH[1][:, 0:3 * NT].rearrange("p (v t) -> p v t", v=3)))
            step(v.tensor_scalar(unf[:, :], tab[:, 0, :], 0.0, trash_id[:, 0:1], ALU.is_equal, ALU.mult))
            v.tensor_scalar(gather_id, tab[:, 0, :], -1.0, 0.0, ALU.add, ALU.max).then_inc(s["idx_s"], 1)
            v.scalar_tensor_tensor(out=add_id, in0=unf[:, :], scalar=-1.0, in1=tab[:, 0, :],
                                   op0=ALU.add, op1=ALU.add).then_inc(s["idx_s"], 1)
            step(v.tensor_tensor(slot_w, tab[:, 1, :], tab[:, 2, :], ALU.add))
            v.wait_ge(s["gate_t_s"], 1)
            v.tensor_scalar(slot_w, slot_w, gates_t[:, 1:2], 1.0 / WSCALE, ALU.mult, ALU.mult).then_inc(s["idx_s"], 1)
            for e in range(EARLY, E):
                split_low(e)

            def low_x(t):
                v.wait_ge(s["x_hi_s"], t + 1)
                v.tensor_tensor(x_lo[:, :, :].rearrange("p k m -> p (k m)"), pA[0][:, :],
                                x_hi[:, :, :].rearrange("p k m -> p (k m)"), ALU.subtract).then_inc(s["x_lo_s"], 1)

            def tile(t, more=True):
                v.wait_ge(s["gate_s_s"], t + 1)
                v.wait_ge(s["pTt"], t)
                v.scalar_tensor_tensor(out=h[:, 0:H], in0=pH[1][:, 0:H], scalar=1.0 / WSCALE, in1=gate_s[:, :],
                                       op0=ALU.mult, op1=ALU.mult).then_inc(s["h_ready"], 1)
                if more:
                    low_x(t + 1)
                v.wait_ge(s["h_hi_s"], t + 1)
                v.tensor_tensor(h_lo[:, :, :].rearrange("p k m -> p (k m)"), pB[0][:, 0:HP],
                                h_hi[:, :, :].rearrange("p k m -> p (k m)"), ALU.subtract).then_inc(s["h_lo_s"], 1)

            low_x(0)
            with v.Fori(0, NT - 1) as t:
                tile(t)
            tile(NT - 1, more=False)


        @block.scalar
        def _(act):
            def split_high(e):
                for n, (lo, hi) in enumerate(PIECES):
                    act.wait_ge(wl[n], 16 * (e + 1))
                    act.activation(piece(w_hi, e, n), w_stage[n][:, :], ACT.Copy, scale=WSCALE).then_inc(s["whi_s"], 1)

            def first_broadcast(b):
                wait(act, "tA", NA * b + 5)
                wait(act, "xs_s", (T - XV) * b)
                wait(act, "xsv_s", XV * b)
                act.activation(inv_bc[:, :], pA[0][:, :], ACT.Copy).then_inc(s["invbc_s"], 1)
                wait(act, "tA", NA * b + 6)
                wait(act, "ws_s", T * b)
                act.activation(s_bc[:, :], pA[1][:, :], ACT.Copy).then_inc(s["sbc_s"], 1)

            def first_quant_rows(b):
                wait(act, "mm1", T * b)
                for k in range(KD):
                    wait(act, "tA", NA * b + 7 + k)
                    act.activation(xqT[:, k, :], pA[k % 2][:, :], ACT.Copy, bias=-ROUND).then_inc(s["xqT_s"], 1)

            def first_quant(b):
                wait(act, "wrq_s", b + 1)
                for t in range(T):
                    act.activation(w_in[:, t, :], w_in[:, t, :], ACT.Identity, bias=round_col[:, 0:1],
                                   scale=w_rq[:, t:t + 1]).then_inc(s["wq_s"], 1)
                for k in range(KD):
                    wait(act, "tA", NA * b + 11 + k)
                    act.activation(wqT[:, k, :], pA[k % 2][:, :], ACT.Copy, bias=-ROUND).then_inc(s["wqT_s"], 1)
                wait(act, "tA", NA * b + 15)
                wait(act, "h_s", T * b)
                act.activation(wsc_bc[:, :], pA[0][:, :], ACT.Copy).then_inc(s["wscbc_s"], 1)

            def first_silu(b, tiles):
                for t in tiles:
                    wait(act, "h_s", T * b + t + 1)
                    wait(act, "a_s", T * b + t - 1)
                    act.activation(silu_g[t % 2], h_buf[:, t % 2, 0:I], ACT.Silu).then_inc(s["silu_s"], 1)

            def second_broadcast(b):
                wait(act, "tB", NB * b + 3)
                wait(act, "as_s", T * b)
                wait(act, "cs_s", T * b)
                act.activation(is2_bc[:, :, :].rearrange("p a i -> p (a i)"), pB[0][:, :], ACT.Copy).then_inc(s["is2_s"], 1)

            def second_quant_rows(b):
                wait(act, "mm2", T * b)
                for k in range(KI):
                    wait(act, "tB", NB * b + 4 + k)
                    act.activation(aqT[:, k, :], pB[(3 + k) % 2][:, :], ACT.Copy, bias=-ROUND).then_inc(s["aqT_s"], 1)

            def second_quant(b):
                wait(act, "crq_s", b + 1)
                for t in range(T):
                    act.activation(c_in[:, t, :], c_in[:, t, :], ACT.Identity, bias=round_col[:, 0:1],
                                   scale=c_rq[:, t:t + 1]).then_inc(s["cq_s"], 1)
                for k in range(KI):
                    wait(act, "tB", NB * b + 6 + k)
                    act.activation(cqT[:, k, :], pB[(5 + k) % 2][:, :], ACT.Copy, bias=-ROUND).then_inc(s["cqT_s"], 1)
                wait(act, "tB", NB * b + 8)
                wait(act, "y_s", T * b)
                act.activation(csc_bc[:, :], pB[1][:, :], ACT.Identity, scale=gates_t[:, 0:1]).then_inc(s["cscbc_s"], 1)

            def rows_of(dram, b):
                return dram[bass.ds(b * S, S), :].rearrange("(t p) d -> p t d", p=P)

            def store_residual(b):
                wait(act, "res_s", T * (b + 1))
                act.dma_start(rows_of(rows, b), x_res).then_inc(s["x_out_s"], 16)

            def store_rows(b):
                wait(act, "xn2_s", T * (b + 1))
                act.dma_start(rows_of(xn2_rows, b), xn2).then_inc(s["xn2_out_s"], 16)

            def second_rows(b, tiles):
                for t in tiles:
                    wait(act, "tB", NB * b + 9 + t)
                    wait(act, "logits", b)
                    act.activation(xn2T[:, t, :, :].rearrange("p k m -> p (k m)"), pB[(8 + t) % 2][:, :],
                                   ACT.Copy).then_inc(s["xn2T_s"], 1)

            def second_logits(b):
                wait(act, "logits", b + 1)
                act.activation(logits, pY[0][0:E, :], ACT.Copy).then_inc(s["logits_s"], 1)

            act.wait_ge(s["g_in_s"], 32)
            act.activation(gates_t[:, :], gates[:, :], ACT.Tanh).then_inc(s["gate_t_s"], 1)
            act.wait_ge(s["consts_a"], N_CONST)
            act.wait_ge(s["gate_t_s"], 1)
            first_broadcast(0)
            split_high(0)
            first_quant_rows(0)
            first_quant(0)
            first_silu(0, range(T))
            second_broadcast(0)
            first_broadcast(1)
            split_high(1)

            def both(b, more=True):
                split_high(b + 1)
                second_quant_rows(b - 1)
                first_quant_rows(b)
                second_quant(b - 1)
                first_quant(b)
                store_residual(b - 1)
                second_rows(b - 1, range(2))
                first_silu(b, range(2))
                second_rows(b - 1, range(2, T))
                first_silu(b, range(2, T))
                store_rows(b - 1)
                second_logits(b - 1)
                second_broadcast(b)
                if more:
                    first_broadcast(b + 1)

            with act.Fori(1, B - 1) as b:
                both(b)
            both(B - 1, more=False)
            b = B - 1
            second_quant_rows(b)
            second_quant(b)
            store_residual(b)
            second_rows(b, range(T))
            store_rows(b)
            second_logits(b)

            act.wait_ge(s["used_s"], 1)
            act.wait_ge(s["rt"], 12)
            act.activation(ex, gap, ACT.Exp).then_inc(s["exp_s"], 1)
            act.wait_ge(s["x_out_s"], 16 * B)
            act.wait_ge(s["xn2_out_s"], 16 * B)
            act.wait_ge(s["router"], B)
            for e in range(EARLY, E):
                split_high(e)

            def high_x(t):
                act.wait_ge(s["pXt"], t + 1)
                act.activation(x_hi[:, :, :].rearrange("p k m -> p (k m)"), pA[0][:, :], ACT.Copy).then_inc(s["x_hi_s"], 1)

            def gate(t):
                act.wait_ge(s["up"], t + 1)
                wait(act, "h_ready", t)
                act.activation(gate_s[:, :], pH[0][:, 0:H], ACT.Silu, scale=1.0 / WSCALE).then_inc(s["gate_s_s"], 1)

            def high_h(t):
                act.wait_ge(s["pTt"], t + 1)
                act.activation(h_hi[:, :, :].rearrange("p k m -> p (k m)"), pB[0][:, 0:HP], ACT.Copy).then_inc(s["h_hi_s"], 1)

            def weigh(t, j, free):
                act.wait_ge(s["down"], t + 1)
                if free is not None:
                    act.wait_ge(added[j], free)
                act.activation(y_out[:, j, :], pY[0][:, :], ACT.Copy, scale=slot_w[:, bass.ds(t, 1)]).then_inc(s["y_ready"], 1)

            act.wait_ge(s["idx_s"], 3)
            act.wait_ge(s["table"], 1)
            high_x(0)
            gate(0)
            high_x(1)
            high_h(0)
            turns = NT // XG - 1
            with act.Fori(0, turns) as i:
                for j in range(1, XG + 1):
                    t = i * XG + j
                    gate(t)
                    high_x(t + 1)
                    weigh(t - 1, j - 1, i * 16)
                    high_h(t)
            for t in range(turns * XG + 1, NT):
                gate(t)
                if t + 1 < NT:
                    high_x(t + 1)
                weigh(t - 1, (t - 1) % XG, turns * 16)
                high_h(t)
            weigh(NT - 1, (NT - 1) % XG, turns * 16)

        @block.tensor
        def _(pe):
            def transpose_chunk(out, src, k):
                for t in range(T):
                    last = pe.transpose(out[:, t * P:(t + 1) * P], src[:, t, k * P:(k + 1) * P], ident[:, :])
                return last

            def broadcast_cols(out, cols, n_cols):
                for k in range(n_cols):
                    last = pe.transpose(out[:, k * P:(k + 1) * P], cols[:, k:k + 1].to_broadcast([P, P]), ident[:, :])
                return last

            def first_cols(b, chunks):
                for k in chunks:
                    if k == 0:
                        wait(pe, "xn_s", T * (b + 1))
                    if k == 0:
                        wait(pe, "h_s", T * b)
                    elif k >= 2:
                        wait(pe, "ax_s", KD * b + k - 1)
                    transpose_chunk(pA[k % 2], xn, k).then_inc(s["tA"], 1)

            def first_broadcasts(b):
                wait(pe, "sinv_s", b + 1)
                wait(pe, "ax_s", KD * (b + 1))
                broadcast_cols(pA[0], s_inv, KD).then_inc(s["tA"], 1)
                broadcast_cols(pA[1], s_col, KD).then_inc(s["tA"], 1)

            def first_rows(b):
                wait(pe, "xq_s", T * (b + 1))
                for k in range(KD):
                    if k == 0:
                        wait(pe, "invbc_s", b + 1)
                    elif k == 1:
                        wait(pe, "sbc_s", b + 1)
                    else:
                        wait(pe, "xqT_s", KD * b + k - 1)
                    transpose_chunk(pA[k % 2], xn, k).then_inc(s["tA"], 1)

            def first_weights(b):
                wait(pe, "wq_s", T * (b + 1))
                for k in range(KD):
                    if k < 2:
                        wait(pe, "xqT_s", KD * b + 3 + k)
                    else:
                        wait(pe, "wqT_s", KD * b + k - 1)
                    transpose_chunk(pA[k % 2], w_in, k).then_inc(s["tA"], 1)
                wait(pe, "wqT_s", KD * b + 3)
                broadcast_cols(pA[0], w_sc, T).then_inc(s["tA"], 1)

            def first_products(b):
                wait(pe, "wqT_s", KD * (b + 1))
                for t in range(T):
                    if t == T - 1:
                        wait(pe, "wscbc_s", b + 1)
                    for k in range(KD):
                        last = pe.matmul(h_bank(t)[:, :], xqT[:, k, t * P:(t + 1) * P], wqT[:, k, :],
                                         start=(k == 0), stop=(k == KD - 1))
                    last.then_inc(s["mm1"], 1)

            def second_cols(b):
                wait(pe, "a_s", T * (b + 1))
                wait(pe, "xn2T_s", T * b)
                for k in range(KI):
                    transpose_chunk(pB[k % 2], a, k).then_inc(s["tB"], 1)

            def second_broadcasts(b):
                wait(pe, "s2inv_s", b + 1)
                broadcast_cols(pB[0][:, 0:I], s2_inv, KI)
                broadcast_cols(pB[0][:, I:2 * I], s2_col, KI).then_inc(s["tB"], 1)

            def second_turn_rows(b):
                wait(pe, "aq_s", T * (b + 1))
                wait(pe, "aa_s", KI * (b + 1))
                transpose_chunk(pB[1], a, 0).then_inc(s["tB"], 1)
                wait(pe, "is2_s", b + 1)
                transpose_chunk(pB[0], a, 1).then_inc(s["tB"], 1)

            def second_turns(b):
                wait(pe, "cq_s", T * (b + 1))
                wait(pe, "aqT_s", KI * b + 1)
                transpose_chunk(pB[1], c_in, 0).then_inc(s["tB"], 1)
                wait(pe, "aqT_s", KI * b + 2)
                transpose_chunk(pB[0], c_in, 1).then_inc(s["tB"], 1)
                wait(pe, "cqT_s", KI * b + 1)
                broadcast_cols(pB[1], c_sc, T).then_inc(s["tB"], 1)

            def second_products(b):
                wait(pe, "cqT_s", KI * (b + 1))
                for t in range(T):
                    if t == 0:
                        wait(pe, "logits_s", b)
                    elif t == 1:
                        wait(pe, "score_s", b)
                    else:
                        wait(pe, "y_s", T * b + t - 1)
                    for k in range(KI):
                        last = pe.matmul(pY[t % 2][:, :], aqT[:, k, t * P:(t + 1) * P], cqT[:, k, :],
                                         start=(k == 0), stop=(k == KI - 1))
                    last.then_inc(s["mm2"], 1)

            def second_router(b):
                for t in range(T + 1):
                    if t < T:
                        wait(pe, "xn2_s", T * b + t + 1)
                        if t == 0:
                            wait(pe, "cqT_s", KI * (b + 1))
                        elif t == 1:
                            wait(pe, "cscbc_s", b + 1)
                        else:
                            wait(pe, "xn2T_s", T * b + t - 1)
                        for k in range(KD):
                            last = pe.transpose(pB[(8 + t) % 2][:, k * P:(k + 1) * P], xn2[:, t, k * P:(k + 1) * P],
                                                ident[:, :])
                        last.then_inc(s["tB"], 1)
                    if t > 0:
                        wait(pe, "xn2T_s", T * b + t)
                        for k in range(KD):
                            last = pe.matmul(pY[0][0:E, (t - 1) * P:t * P], wgT[:, k, :], xn2T[:, t - 1, k, :],
                                             start=(k == 0), stop=(k == KD - 1))
                last.then_inc(s["logits"], 1)

            def second_scores(b):
                if isinstance(b, int):
                    wait(pe, "logits_s", b + 1)
                for t in range(T):
                    last = pe.transpose(pY[1][:, t * E:(t + 1) * E], logits[:, t * P:(t + 1) * P], ident[0:E, 0:E])
                last.then_inc(s["router"], 1)

            pe.wait_ge(s["consts_a"], N_CONST)
            first_cols(0, range(KD))
            first_broadcasts(0)
            first_rows(0)
            first_weights(0)
            first_products(0)
            second_cols(0)
            first_cols(1, range(KD))
            second_broadcasts(0)
            first_broadcasts(1)
            pe.wait_ge(s["wg_in_s"], 16)

            def both(b, more=True):
                second_turn_rows(b - 1)
                first_rows(b)
                second_turns(b - 1)
                second_products(b - 1)
                first_weights(b)
                first_products(b)
                second_router(b - 1)
                second_cols(b)
                if more:
                    first_cols(b + 1, range(KD - 1))
                    wait(pe, "logits_s", b)
                    first_cols(b + 1, range(KD - 1, KD))
                second_scores(b - 1)
                second_broadcasts(b)
                if more:
                    first_broadcasts(b + 1)

            with pe.Fori(1, B - 1) as b:
                both(b)
            both(B - 1, more=False)
            b = B - 1
            second_turn_rows(b)
            second_turns(b)
            second_products(b)
            second_router(b)
            second_scores(b)

            pe.wait_ge(s["used_s"], 1)
            used_all = used[:, :, :].rearrange("p i e -> p (i e)")
            pe.matmul(pH[0][:, 0:(NTOK + 1) * E], before[:, :], used_all, start=True, stop=False)
            for i in range(NTOK):
                last = pe.matmul(pH[0][:, (i + 1) * E:(NTOK + 1) * E], ones[:, :],
                                 used[:, i:i + 1, :].to_broadcast([P, NTOK - i, E]), start=False, stop=(i == NTOK - 1))
            last.then_inc(s["prefix"], 1)
            pe.wait_ge(s["table_free"], 1)
            for j in range(TOPK * NTOK):
                last = pe.matmul(pH[1][:, 0:3 * NT], in_slot[:, j, :], entry[:, j, :, :].rearrange("p v t -> p (v t)"),
                                 start=(j == 0), stop=(j == TOPK * NTOK - 1))
            last.then_inc(s["table"], 1)

            def turn_x(t, j, count):
                pe.wait_ge(gathered[j], count)
                wait(pe, "x_lo_s", t)
                for k in range(KD):
                    last = pe.transpose(pA[0][:, k * P:(k + 1) * P], xg[:, j, k * P:(k + 1) * P], ident[:, :])
                last.then_inc(s["pXt"], 1)

            def weights(half, e, lo, hi):
                return half[:, bass.ds(e, 1), lo:hi].rearrange("p a n -> p (a n)")

            def up(t, e):
                pe.wait_ge(s["x_lo_s"], t + 1)
                wait(pe, "h_ready", t)
                for part in range(2):
                    for k in range(KD):
                        lo = k * 2 * H + part * H
                        for m, (xs, ws) in enumerate(((x_hi, w_hi), (x_hi, w_lo), (x_lo, w_hi))):
                            last = pe.matmul(pH[part][:, 0:H], xs[:, k, :], weights(ws, e, lo, lo + H),
                                             start=(k == 0 and m == 0), stop=(k == KD - 1 and m == 2))
                last.then_inc(s["up"], 1)

            def turn_h(t):
                pe.wait_ge(s["h_ready"], t + 1)
                wait(pe, "h_lo_s", t)
                for k in range(KH):
                    last = pe.transpose(pB[0][:, k * P:(k + 1) * P], h[:, k * P:(k + 1) * P], ident[:, :])
                last.then_inc(s["pTt"], 1)

            def down(t, e):
                pe.wait_ge(s["h_lo_s"], t + 1)
                wait(pe, "y_ready", t)
                for k in range(KH):
                    lo = WU + k * D
                    for m, (hs, ws) in enumerate(((h_hi, w_hi), (h_hi, w_lo), (h_lo, w_hi))):
                        last = pe.matmul(pY[0][:, :], hs[:, k, :], weights(ws, e, lo, lo + D),
                                         start=(k == 0 and m == 0), stop=(k == KH - 1 and m == 2))
                last.then_inc(s["down"], 1)

            def expert(t):
                return pe.value_load(te[0:1, bass.ds(t, 1)], min_val=0, max_val=E - 1)

            pe.wait_ge(s["te_s"], 1)
            pe.wait_ge(s["h_pad_s"], 1)
            pe.wait_ge(s["idx_s"], 3)
            pe.wait_ge(s["wlo_s"], 2 * E)
            turn_x(0, 0, 16)
            up(0, expert(0))
            turn_x(1, 1, 16)
            turn_h(0)
            turns = NT // XG - 1
            with pe.Fori(0, turns) as i:
                for j in range(1, XG + 1):
                    t = i * XG + j
                    up(t, expert(t))
                    turn_x(t + 1, (j + 1) % XG, (i + (j + 1) // XG + 1) * 16)
                    down(t - 1, expert(t - 1))
                    turn_h(t)
            for t in range(turns * XG + 1, NT):
                up(t, expert(t))
                if t + 1 < NT:
                    turn_x(t + 1, (t + 1) % XG, ((t + 1) // XG + 1) * 16)
                down(t - 1, expert(t - 1))
                turn_h(t)
            down(NT - 1, expert(NT - 1))


def kernel(x, fside_BxS2xS2_0, ctx_1024, g_xattn, g_ffn, L0_ffn_Wg, L0_ffn_W1, L0_ffn_W2, L0_ffn_W3):
    import numpy as np
    import concourse.bacc as bacc
    from concourse.bass_utils import run_bass_kernel_spmd

    def tiles(m):
        m = np.asarray(m)
        return np.ascontiguousarray(m.reshape(m.shape[0], m.shape[1] // P, P, m.shape[2]).transpose(0, 2, 1, 3))

    def turned(m):
        return tiles(np.asarray(m).transpose(0, 2, 1))

    w3 = np.zeros((E, HP, D), np.float32)
    w3[:, :H, :] = np.asarray(L0_ffn_W3).transpose(0, 2, 1)
    up = np.concatenate([np.asarray(L0_ffn_W1), np.asarray(L0_ffn_W2)], axis=1)
    wexp = np.concatenate([turned(up).reshape(E, P, WU), tiles(w3).reshape(E, P, KH * D)], axis=2)
    arrays = {
        "x_t": tiles(x),
        "w_t": tiles(fside_BxS2xS2_0), "w_turned": turned(fside_BxS2xS2_0),
        "c_t": tiles(ctx_1024), "c_turned": turned(ctx_1024),
        "g_x": np.asarray(g_xattn).reshape(1, 1), "g_f": np.asarray(g_ffn).reshape(1, 1),
        "wg_t": turned(np.asarray(L0_ffn_Wg)[None])[0],
        "wexp": np.ascontiguousarray(wexp),
    }
    nc = bacc.Bacc("TRN2", target_bir_lowering=False, num_devices=1)
    aps = [nc.dram_tensor(k, v.shape, mybir.dt.from_np(v.dtype), kind="ExternalInput").ap() for k, v in arrays.items()]
    rows = nc.dram_tensor("rows", (ROWS + P, D), F32, kind="ExternalOutput").ap()
    xn2_rows = nc.dram_tensor("xn2_rows", (ROWS, D), F32).ap()
    build_program(nc, *aps, rows, xn2_rows)
    r = run_bass_kernel_spmd(nc, [arrays], core_ids=[0])
    return r.results[0]["rows"][:ROWS].reshape(B, S, D)
```

```python
from contextlib import ExitStack

import concourse.bass as bass
from concourse import mybir

F32 = mybir.dt.float32
F16 = mybir.dt.float16
BF16 = mybir.dt.bfloat16
I32 = mybir.dt.int32
U32 = mybir.dt.uint32
ALU = mybir.AluOpType
ACT = mybir.ActivationFunctionType
X = mybir.AxisListType.X

P = 128
B, S, D = 4, 512, 512
I = 256
T = S // P
KD = D // P
KI = I // P
E, H, TOPK = 8, 352, 2
KH = -(-H // P)
HP = KH * P
NTOK = B * T
ROWS = B * S
NT = (TOPK * ROWS - E) // P + E
TRASH = ROWS
WU = KD * 2 * H
WE = WU + KH * D
NB = 12
NA = 15
XV = 2
WV = 2
N_CONST = 13
LATE = 3
EARLY = E - LATE
GAP_STEP = 6 * TOPK

EPS_LN = 1e-5
EPS = 1e-6
QMAX = 127.0
ROUND = 1.5 * 2.0 ** 23
WSCALE = 256.0
BIG = 3.0e38


def build_program(nc, x, w, wT, c, cT, g_x, g_f, wg, wexp, rows, xn2_rows):
    with ExitStack() as ctx:
        def sb(name, shape, dt):
            return ctx.enter_context(nc.sbuf_tensor(name, shape, dt))

        def bank(name):
            return ctx.enter_context(nc.psum_tensor(name, [P, 512], F32))

        def sem(name):
            return ctx.enter_context(nc.semaphore(name))

        w_hi = sb("w_hi", [P, E, WE], F16)
        w_lo = sb("w_lo", [P, E, WE], F16)
        w_stage = [sb("w_stage0", [P, WU], F32), sb("w_stage1", [P, WE - WU], F32)]

        hi_space = w_hi[:, EARLY:E, :].rearrange("p e n -> p (e n)").bitcast(F32)
        lo_space = w_lo[:, EARLY:E, :].rearrange("p e n -> p (e n)").bitcast(F32)
        n = T * D
        w_in = hi_space[:, 0:n].rearrange("p (t d) -> p t d", t=T)
        wT_in = hi_space[:, n:2 * n].rearrange("p (t d) -> p t d", t=KD)
        silu_g = [hi_space[:, 2 * n:2 * n + I], lo_space[:, n:n + I]]
        x_res = hi_space[:, 2 * n + I:3 * n + I].rearrange("p (t d) -> p t d", t=T)
        c_in = lo_space[:, 0:T * I].rearrange("p (t d) -> p t d", t=T)
        cT_in = lo_space[:, T * I:2 * T * I].rearrange("p (k o) -> p k o", k=KI)
        xn2 = lo_space[:, n + I:2 * n + I].rearrange("p (t d) -> p t d", t=T)
        xn2T = lo_space[:, 2 * n + I:3 * n + I].rearrange("p (t k m) -> p t k m", t=T, k=KD)

        x_in = sb("x_in", [P, T, D], F32)
        xn = sb("xn", [P, T, D], F32)
        wqT = sb("wqT", [P, KD, D], BF16)
        a = sb("a", [P, T, I], F32)
        csc_bc = sb("csc_bc", [P, D], F32)
        first_space = sb("first_space", [P, KD * S // 2 + 3 * D + 4 * I], F32)
        n = KD * S // 2
        xqT = first_space[:, 0:n].bitcast(BF16).rearrange("p (k m) -> p k m", k=KD)
        inv_bc, s_bc, wsc_bc = (first_space[:, n + i * D:n + (i + 1) * D] for i in range(3))
        n += 3 * D
        h_buf = first_space[:, n:n + 4 * I].rearrange("p (a i) -> p a i", a=2)
        second_space = sb("second_space", [P, WE - WU], F32)
        n = KI * S // 2
        aqT = second_space[:, 0:n].bitcast(BF16).rearrange("p (k m) -> p k m", k=KI)
        cqT = second_space[:, n:2 * n].bitcast(BF16).rearrange("p (k m) -> p k m", k=KI)
        is2_bc = second_space[:, 2 * n:2 * n + 2 * I].rearrange("p (a i) -> p a i", a=2)
        y_tmp = sb("y_tmp", [P, 2, D], F32)

        logits = y_tmp[0:E, 1, :]

        def small(name, *shape):
            return sb(name, [P, *shape], F32)

        x_st, x_mv, x_var, x_rstd = small("x_st", T, 6), small("x_mv", T, 2), small("x_var", T), small("x_rstd", T)
        r_st, r_mv, r_var, r_rstd = small("r_st", T, 6), small("r_mv", T, 2), small("r_var", T), small("r_rstd", T)
        aw, aw_c, aw_r, ax = small("aw", KD), small("aw_c", KD), small("aw_r", KD), small("ax", KD)
        ratio, s_raw, s_col, s_inv = small("ratio", KD), small("s_raw", KD), small("s_col", KD), small("s_inv", KD)
        xs_max, x_sc, x_rq = small("xs_max", T), small("x_sc", T), small("x_rq", T)
        ws_max, w_sc, w_rq = small("ws_max", T), small("w_sc", T), small("w_rq", T)
        ac, ac_c, ac_r, aa = small("ac", KI), small("ac_c", KI), small("ac_r", KI), small("aa", KI)
        ratio2, s2_raw, s2_col, s2_inv = small("ratio2", KI), small("s2_raw", KI), small("s2_col", KI), small("s2_inv", KI)
        as_max, a_sc, a_rq = small("as_max", T), small("a_sc", T), small("a_rq", T)
        cs_max, c_sc, c_rq = small("cs_max", T), small("c_sc", T), small("c_rq", T)
        half, minus_half, round_col = small("half", T), small("minus_half", T), small("round_col", 1)
        gates, gates_t, spare = small("gates", 2), small("gates_t", 2), small("spare", 1)
        wgT = small("wgT", KD, E)
        ident = small("ident", P)

        scores = small("scores", NTOK, E)
        a_flat = a[:, :, :].rearrange("p t i -> p (t i)")
        ne = NTOK * E
        pref = small("pref", E)
        ohs = a_flat[:, 0:TOPK * ne].rearrange("p (k i e) -> p k i e", k=TOPK, e=E)
        tmp_e, sc2, pos_e = (a_flat[:, (TOPK + i) * ne:(TOPK + i + 1) * ne].rearrange("p (i e) -> p i e", e=E) for i in range(3))
        late_t = a_flat[:, (TOPK + 3) * ne:(TOPK + 3) * ne + NT * E].rearrange("p (t e) -> p t e", e=E)
        h_flat = first_space[:, WU:]

        def pair(i):
            return h_flat[:, i * TOPK * NTOK:(i + 1) * TOPK * NTOK].rearrange("p (k i) -> p k i", k=TOPK)

        top, pick, prob, pos, tile_of, slot_of, tile_x = (pair(i) for i in range(7))
        gap, ex, den = pair(7)[:, 0, :], pair(7)[:, 1, :], pair(8)[:, 0, :]
        row_no, prob_lo = pair(9), pair(10)
        at = 11 * TOPK * NTOK
        tab = h_flat[:, at:at + 3 * NT].rearrange("p (v t) -> p v t", v=3)
        te_f = h_flat[:, at + 3 * NT:at + 4 * NT]
        unf = h_flat[:, at + 4 * NT:at + 5 * NT]
        used = sb("used", [P, NTOK + 1, E], BF16)
        before = sb("before", [P, P], BF16)
        ones = sb("ones", [P, P], BF16)
        n_tiles, n_ends, n_starts, ones_e = small("n_tiles", E), small("n_ends", E), small("n_starts", E), small("ones_e", E)
        p_hi = sb("p_hi", [P, TOPK, NTOK], F16)
        iota_p = small("iota_p", P)
        iota_t = small("iota_t", NT)
        row_id = small("row_id", NTOK)
        trash_id = small("trash_id", 1)
        te = sb("te", [P, NT], I32)
        gather_id = y_tmp[:, 0, NT:2 * NT].bitcast(U32)
        add_id = y_tmp[:, 0, 2 * NT:3 * NT].bitcast(U32)
        slot_w = y_tmp[:, 0, 0:NT]
        zeros = x_in[:, 0, :]
        in_slot = x_in[:, :, :].rearrange("p t d -> p (t d)").bitcast(F16)[:, 0:TOPK * NTOK * P].rearrange("p (j m) -> p j m", m=P)
        row_entry = xn[:, :, :].rearrange("p t d -> p (t d)").bitcast(F16)[:, 0:TOPK * NTOK * NT].rearrange(
            "p (j t) -> p j t", t=NT)
        prob_entry = second_space[:, :].bitcast(F16)[:, 0:TOPK * NTOK * 2 * NT].rearrange("p (j v t) -> p j v t", v=2, t=NT)
        in_tile = wqT[:, :, :].rearrange("p t d -> p (t d)").bitcast(F16)[:, 0:TOPK * NTOK * NT].rearrange(
            "p (j t) -> p j t", t=NT)

        XG = 3
        xg = xn[:, 0:XG, :]
        y_out = x_in[:, 0:XG, :]
        x_hi = inv_bc[:, :].bitcast(F16)[:, 0:D].rearrange("p (k m) -> p k m", k=KD)
        x_lo = inv_bc[:, :].bitcast(F16)[:, D:2 * D].rearrange("p (k m) -> p k m", k=KD)
        gate_s = wsc_bc[:, 0:H]
        h = csc_bc[:, 0:HP]
        h_hi = s_bc[:, :].bitcast(F16)[:, 0:HP].rearrange("p (k m) -> p k m", k=KH)
        h_lo = s_bc[:, :].bitcast(F16)[:, HP:2 * HP].rearrange("p (k m) -> p k m", k=KH)
        AHEAD = XG + 2
        turn_ix = sb("turn_ix", [P, XG, 2], U32)
        turn_id = y_tmp[:, 0, NT + AHEAD:3 * NT - AHEAD].rearrange("p (v t) -> p v t", v=2).bitcast(U32)

        pA = [bank("pA0"), bank("pA1")]
        pB = [bank("pB0"), bank("pB1")]
        pH = [bank("pH0"), bank("pH1")]
        pY = [bank("pY0"), bank("pY1")]

        def h_bank(t):
            return pH[t] if t < 2 else pA[3 - t]

        names = """consts_a consts_v consts_m x_in_s w_in_s wT_in_s c_in_s cT_in_s res_in_s g_in_s wg_in_s zero_s
            x_stats x_aggr x_var_s x_rstd_s xn_s aw_s awc_s awr_s ax_s ratio_s sraw_s scol_s sinv_s xsv_s wqv_s
            invbc_s sbc_s xs_s ws_s xsmax_s xsc_s xrq_s wsmax_s wsc_s wrq_s xq_s wq_s
            tA tA_v tA_a wqT_s xqT_s wscbc_s mm1 h_s silu_s a_s
            ac_s acc_s acr_s aa_s ratio2_s s2raw_s s2col_s s2inv_s is2_s as_s cs_s asmax_s asc_s arq_s
            csmax_s csc_s crq_s aq_s cq_s tB tB_v tB_a cqT_s aqT_s cscbc_s mm2 y_s res_s
            r_stats r_aggr r_var_s r_rstd_s xn2_s xn2T_s logits logits_s router score_s x_out_s xn2_out_s gate_t_s
            wl0 wl1 wl0_late wl1_late whi_s wlo_s whi_g w_scaled wlo_g
            rt exp_s used_s prefix table idx_s te_s table_free
            h_pad_s ix_s gather0 gather1 gather2 pXt x_hi_s x_lo_s up gate_s_s h_ready pTt h_hi_s h_lo_s down y_ready add0 add1 add2 init_s"""
        s = {k: sem(k) for k in names.split()}
        wl = [s["wl0"], s["wl1"]]
        wl_late = [s["wl0_late"], s["wl1_late"]]
        gathered = [s["gather0"], s["gather1"], s["gather2"]]
        added = [s["add0"], s["add1"], s["add2"]]

        def wait(eng, name, count):
            if not (isinstance(count, int) and count <= 0):
                eng.wait_ge(s[name] if isinstance(name, str) else name, count)

        PIECES = [(0, WU), (WU, WE)]
        late_stage = [first_space[:, 0:WU], second_space[:, :]]

        def stage_of(e):
            return late_stage if isinstance(e, int) and e == E - 2 else [w_stage[0][:, :], w_stage[1][:, :]]

        GPSIMD_SPLITS = [*range(1, B), E - 2, E - 1]
        VECTOR_SPLITS = [e for e in range(E) if e not in GPSIMD_SPLITS]

        def low_count(e, n):
            if not isinstance(e, int):
                return 2 * (e - 1) + n + 1
            return 2 * (GPSIMD_SPLITS if e in GPSIMD_SPLITS else VECTOR_SPLITS).index(e) + n + 1

        def piece(half, e, n):
            return half[:, bass.ds(e, 1), PIECES[n][0]:PIECES[n][1]].rearrange("p a n -> p (a n)")

        block = ctx.enter_context(nc.Block())

        @block.sync
        def _(sp):
            def load_w(e):
                for n, (lo, hi) in enumerate(PIECES):
                    before_it = EARLY if e == E - 1 else e - 1
                    if before_it in GPSIMD_SPLITS:
                        wait(sp, "wlo_g", low_count(before_it, n))
                    elif e > 0:
                        wait(sp, "wlo_s", low_count(before_it, n))

                    sp.dma_start(w_stage[n][:, :], wexp[bass.ds(e, 1), :, lo:hi].rearrange("a p n -> p (a n)")
                                 ).then_inc(wl[n], 16)

            def batch(dram, b):
                return dram[bass.ds(b, 1), :, :, :].rearrange("a p t d -> p (a t) d")

            def load_x(b):
                wait(sp, "xn_s", T * b)
                sp.dma_start(x_in[:, :, :], batch(x, b)).then_inc(s["x_in_s"], 16)
                wait(sp, "aw_s", b)
                sp.dma_start(wT_in, batch(wT, b)).then_inc(s["wT_in_s"], 16)

            def load_first(b):
                wait(sp, "wqT_s", KD * b)
                sp.dma_start(w_in, batch(w, b)).then_inc(s["w_in_s"], 16)

            def load_cT(b):
                wait(sp, "ac_s", b)
                sp.dma_start(cT_in, batch(cT, b)).then_inc(s["cT_in_s"], 16)

            def load_c(b):
                wait(sp, "cqT_s", KI * b)
                sp.dma_start(c_in, batch(c, b)).then_inc(s["c_in_s"], 16)

            def load_residual(b):
                wait(sp, "x_out_s", 16 * b)
                wait(sp, "xn2_s", T * b)
                sp.dma_start(x_res, batch(x, b)).then_inc(s["res_in_s"], 16)

            load_x(0)
            load_first(0)
            sp.dma_start(gates[:, 0:1], g_x.to_broadcast([P, 1])).then_inc(s["g_in_s"], 16)
            sp.dma_start(gates[:, 1:2], g_f.to_broadcast([P, 1])).then_inc(s["g_in_s"], 16)
            sp.dma_start(wgT[:, :, :], wg).then_inc(s["wg_in_s"], 16)
            load_cT(0)
            load_w(0)
            load_x(1)
            load_c(0)
            load_residual(0)
            load_w(1)
            load_first(1)
            for b in range(1, B):
                if b + 1 < B:
                    load_x(b + 1)
                load_cT(b)
                load_c(b)
                if b + 1 < B:
                    load_first(b + 1)
                load_w(b + 1)
                load_residual(b)
            wait(sp, "zero_s", 1)
            sp.dma_start(rows[TRASH:TRASH + P, :], zeros).then_inc(s["init_s"], 16)
            wait(sp, "a_s", T * B)
            sp.dma_start(late_stage[0], wexp[E - 2, :, 0:WU]).then_inc(wl_late[0], 16)
            load_w(EARLY)
            wait(sp, "mm2", T * B)
            sp.dma_start(late_stage[1], wexp[E - 2, :, WU:WE]).then_inc(wl_late[1], 16)
            wait(sp, "xn2_s", T * B)
            sp.dma_start(xn2_rows[(B - 1) * S:B * S, :].rearrange("(t p) d -> p t d", p=P), xn2).then_inc(s["xn2_out_s"], 16)
            load_w(E - 1)
            sp.wait_ge(s["x_out_s"], 16 * B)
            sp.wait_ge(s["xn2_out_s"], 16 * B)
            sp.wait_ge(s["init_s"], 16)
            for j in range(XG):
                sp.wait_ge(added[j], 16 * len(range(j, NT, XG)))

        @block.gpsimd
        def _(g):
            g.memset(ident[:, :], 0.0).then_inc(s["consts_m"], 1)
            g.memset(before[:, :], 1.0).then_inc(s["consts_m"], 1)
            g.memset(ones[:, :], 1.0).then_inc(s["consts_a"], 1)
            g.memset(half[:, :], 0.5).then_inc(s["consts_a"], 1)
            g.memset(minus_half[:, :], -0.5).then_inc(s["consts_a"], 1)
            g.memset(round_col[:, :], ROUND).then_inc(s["consts_a"], 1)
            g.memset(ones_e[:, :], 1.0).then_inc(s["consts_a"], 1)
            g.memset(used[:, NTOK, :], 0.0).then_inc(s["consts_a"], 1)
            g.wait_ge(s["consts_m"], 2)
            g.affine_select(out=ident[:, :], in_=ident[:, :], compare_op=ALU.not_equal, fill=1.0, base=0,
                            pattern=[[-1, P]], channel_multiplier=1).then_inc(s["consts_a"], 1)
            g.affine_select(out=before[:, :], in_=before[:, :], compare_op=ALU.is_gt, fill=0.0, base=0,
                            pattern=[[1, P]], channel_multiplier=-1).then_inc(s["consts_a"], 1)
            g.iota(pref[:, :], pattern=[[-1, E]], base=E, channel_multiplier=0,
                   allow_small_or_imprecise_dtypes=True).then_inc(s["consts_a"], 1)
            g.iota(iota_p[:, :], pattern=[[1, P]], base=0, channel_multiplier=0,
                   allow_small_or_imprecise_dtypes=True).then_inc(s["consts_a"], 1)
            g.iota(iota_t[:, :], pattern=[[1, NT]], base=0, channel_multiplier=0,
                   allow_small_or_imprecise_dtypes=True).then_inc(s["consts_a"], 1)
            g.iota(row_id[:, :], pattern=[[P, NTOK]], base=1, channel_multiplier=1,
                   allow_small_or_imprecise_dtypes=True).then_inc(s["consts_a"], 1)
            g.iota(trash_id[:, :], pattern=[[0, 1]], base=TRASH + 1, channel_multiplier=1,
                   allow_small_or_imprecise_dtypes=True).then_inc(s["consts_a"], 1)
            g.wait_ge(s["consts_a"], N_CONST)

            def first_rstd(b):
                wait(g, "x_var_s", b + 1)
                g.tensor_tensor(x_rstd[:, :], x_var[:, :], minus_half[:, :], ALU.pow).then_inc(s["x_rstd_s"], 1)

            def first_root(b):
                wait(g, "ratio_s", b + 1)
                g.tensor_tensor(s_raw[:, :], ratio[:, :], half[:, 0:KD], ALU.pow).then_inc(s["sraw_s"], 1)

            def first_scale_x(b):
                wait(g, "invbc_s", b + 1)
                wait(g, "ax_s", KD * (b + 1))
                for t in range(XV, T):
                    g.tensor_tensor(xn[:, t, :], xn[:, t, :], inv_bc[:, :], ALU.mult).then_inc(s["xs_s"], 1)

            def first_scale_w(b):
                wait(g, "sbc_s", b + 1)
                wait(g, "w_in_s", 16 * (b + 1))
                for t in range(T):
                    g.tensor_tensor(w_in[:, t, :], w_in[:, t, :], s_bc[:, :], ALU.mult).then_inc(s["ws_s"], 1)

            def low_piece(e, n):
                wait(g, "w_scaled", low_count(e, n))
                g.tensor_tensor(piece(w_lo, e, n), stage_of(e)[n], piece(w_hi, e, n), ALU.subtract).then_inc(s["wlo_g"], 1)

            def second_root(b):
                wait(g, "ratio2_s", b + 1)
                g.tensor_tensor(s2_raw[:, :], ratio2[:, :], half[:, 0:KI], ALU.pow).then_inc(s["s2raw_s"], 1)

            def second_scale(b):
                wait(g, "is2_s", b + 1)
                wait(g, "aa_s", KI * (b + 1))
                for t in range(T):
                    g.tensor_tensor(a[:, t, :], a[:, t, :], is2_bc[:, 0, :], ALU.mult).then_inc(s["as_s"], 1)

            def second_scale_c(b):
                wait(g, "c_in_s", 16 * (b + 1))
                for t in range(T):
                    g.tensor_tensor(c_in[:, t, :], c_in[:, t, :], is2_bc[:, 1, :], ALU.mult).then_inc(s["cs_s"], 1)

            def residual(b):
                wait(g, "res_in_s", 16 * (b + 1))
                for t in range(T):
                    wait(g, "y_s", T * b + t + 1)
                    g.tensor_tensor(x_res[:, t, :], x_res[:, t, :], y_tmp[:, t % 2, :], ALU.add).then_inc(s["res_s"], 1)

            def second_rstd(b):
                wait(g, "r_var_s", b + 1)
                g.tensor_tensor(r_rstd[:, :], r_var[:, :], minus_half[:, :], ALU.pow).then_inc(s["r_rstd_s"], 1)

            def both(b, more=True):
                second_scale_c(b - 1)
                first_scale_x(b)
                first_scale_w(b)
                residual(b - 1)
                if more:
                    first_rstd(b + 1)
                second_rstd(b - 1)
                if not more:
                    g.wait_ge(s["xn_s"], T * B)
                    g.memset(zeros, 0.0).then_inc(s["zero_s"], 1)
                low_piece(b, 0)
                second_root(b)
                low_piece(b, 1)
                second_scale(b)
                if more:
                    first_root(b + 1)

            first_rstd(0)
            first_root(0)
            first_scale_x(0)
            first_scale_w(0)
            first_rstd(1)
            second_root(0)
            second_scale(0)
            first_root(1)
            with g.Fori(1, B - 1) as b:
                both(b)
            both(B - 1, more=False)
            residual(B - 1)
            second_rstd(B - 1)

            g.wait_ge(s["xn2_out_s"], 16 * B)
            g.wait_ge(s["xn2T_s"], T * B)
            low_piece(E - 2, 0)
            low_piece(E - 2, 1)
            g.wait_ge(s["logits"], B)
            low_piece(E - 1, 0)

            g.wait_ge(s["idx_s"], 2)
            g.wait_ge(s["xn2_out_s"], 16 * B)
            g.wait_ge(s["x_out_s"], 16 * B)
            g.wait_ge(s["init_s"], 16)

            def gather(j, ids):
                g.indirect_dma_start(out=xg[:, j, :], out_offset=None, in_=xn2_rows,
                                     in_offset=bass.IndirectOffsetOnAxis(ap=ids, axis=0)).then_inc(gathered[j], 16)

            def add_rows(j, ids):
                g.indirect_dma_start(out=rows, out_offset=bass.IndirectOffsetOnAxis(ap=ids, axis=0),
                                     in_=y_out[:, j, :], in_offset=None, compute_op=ALU.add).then_inc(added[j], 16)

            def ids_of(t, j):
                g.tensor_copy(turn_ix[:, j, :].rearrange("p (v a) -> p v a", a=1), turn_id[:, :, bass.ds(t, 1)]
                              ).then_inc(s["ix_s"], 1)

            for t in range(AHEAD):
                if t >= XG:
                    g.wait_ge(s["pXt"], t - XG + 1)
                gather(t % XG, gather_id[:, t:t + 1])
                if t == XG - 1:
                    ids_of(0, 0)
            turns = (NT - AHEAD) // XG
            with g.Fori(0, turns) as i:
                for j in range(XG):
                    t = i * XG + j
                    g.wait_ge(s["ix_s"], t + 1)
                    g.wait_ge(s["y_ready"], t + 1)
                    g.wait_ge(gathered[j], (i + 2) * 16)
                    g.wait_ge(added[(j - 1) % XG], (i + (1 if j else 0)) * 16)
                    ids_of(t + 1, (j + 1) % XG)
                    add_rows(j, turn_ix[:, j, 1:2])
                    gather((j + AHEAD) % XG, turn_ix[:, j, 0:1])
            for t in range(turns * XG, NT):
                g.wait_ge(s["y_ready"], t + 1)
                g.wait_ge(added[(t - 1) % XG], ((t - 1) // XG + 1) * 16)
                add_rows(t % XG, add_id[:, t:t + 1])
                if t + AHEAD < NT:
                    gather((t + AHEAD) % XG, gather_id[:, t + AHEAD:t + AHEAD + 1])

        @block.vector
        def _(v):
            def split_low(e):
                for n, (lo, hi) in enumerate(PIECES):
                    wait(v, "whi_s", 2 * e + n + 1)
                    v.scalar_tensor_tensor(out=piece(w_lo, e, n), in0=w_stage[n][:, :], scalar=WSCALE,
                                           in1=piece(w_hi, e, n), op0=ALU.mult, op1=ALU.subtract).then_inc(s["wlo_s"], 1)

            def first_stats(b):
                wait(v, "x_in_s", 16 * (b + 1))
                for t in range(T):
                    v.bn_stats(x_st[:, t, :], x_in[:, t, :]).then_inc(s["x_stats"], 1)
                wait(v, "x_stats", T * (b + 1))
                v.memset(spare[:, :], 0.0)
                for t in range(T):
                    v.bn_aggr(x_mv[:, t, :], x_st[:, t, :]).then_inc(s["x_aggr"], 1)
                wait(v, "x_aggr", T * (b + 1))
                v.tensor_scalar(x_var[:, :], x_mv[:, :, 1], EPS_LN, None, ALU.add).then_inc(s["x_var_s"], 1)

            def first_weight_max(b):
                wait(v, "wT_in_s", 16 * (b + 1))
                v.tensor_reduce(aw[:, :], wT_in, X, ALU.max, apply_absolute_value=True).then_inc(s["aw_s"], 1)
                wait(v, "aw_s", b + 1)
                v.tensor_scalar(aw_c[:, :], aw[:, :], EPS, None, ALU.max).then_inc(s["awc_s"], 1)
                wait(v, "awc_s", b + 1)
                v.reciprocal(aw_r[:, :], aw_c[:, :]).then_inc(s["awr_s"], 1)

            def first_norm(b):
                wait(v, "x_rstd_s", b + 1)
                wait(v, "xqT_s", KD * b)
                for t in range(T):
                    v.tensor_scalar(xn[:, t, :], x_in[:, t, :], x_mv[:, t, 0:1], x_rstd[:, t:t + 1],
                                    ALU.subtract, ALU.mult).then_inc(s["xn_s"], 1)

            def first_col_max(b, chunks):
                for k in chunks:
                    wait(v, "tA", NA * b + k + 1)
                    v.tensor_reduce(ax[:, k:k + 1], pA[k % 2][:, :], X, ALU.max,
                                    apply_absolute_value=True).then_inc(s["ax_s"], 1)

            def first_ratio(b):
                wait(v, "ax_s", KD * (b + 1))
                wait(v, "awr_s", b + 1)
                v.scalar_tensor_tensor(out=ratio[:, :], in0=ax[:, :], scalar=EPS, in1=aw_r[:, :],
                                       op0=ALU.max, op1=ALU.mult).then_inc(s["ratio_s"], 1)

            def first_smooth(b):
                wait(v, "sraw_s", b + 1)
                v.tensor_scalar(s_col[:, :], s_raw[:, :], EPS, None, ALU.max).then_inc(s["scol_s"], 1)
                wait(v, "scol_s", b + 1)
                v.reciprocal(s_inv[:, :], s_col[:, :]).then_inc(s["sinv_s"], 1)

            def first_scale_x(b):
                wait(v, "invbc_s", b + 1)
                for t in range(XV):
                    v.tensor_tensor(xn[:, t, :], xn[:, t, :], inv_bc[:, :], ALU.mult).then_inc(s["xsv_s"], 1)

            def first_row_scale(b):
                wait(v, "xsv_s", XV * (b + 1))
                wait(v, "xs_s", (T - XV) * (b + 1))
                v.tensor_reduce(xs_max[:, :], xn[:, :, :], X, ALU.max, apply_absolute_value=True).then_inc(s["xsmax_s"], 1)
                wait(v, "xsmax_s", b + 1)
                wait(v, "h_s", T * b)
                v.tensor_scalar(x_sc[:, :], xs_max[:, :], EPS, 1.0 / QMAX, ALU.max, ALU.mult).then_inc(s["xsc_s"], 1)
                wait(v, "xsc_s", b + 1)
                v.reciprocal(x_rq[:, :], x_sc[:, :]).then_inc(s["xrq_s"], 1)
                wait(v, "xrq_s", b + 1)
                for t in range(T):
                    v.tensor_scalar(xn[:, t, :], xn[:, t, :], x_rq[:, t:t + 1], ROUND, ALU.mult, ALU.add).then_inc(s["xq_s"], 1)

            def first_weight_scale(b):
                for t in range(0, T, 2):
                    wait(v, "ws_s", T * b + t + 2)
                    v.tensor_reduce(ws_max[:, t:t + 2], w_in[:, t:t + 2, :], X, ALU.max,
                                    apply_absolute_value=True).then_inc(s["wsmax_s"], 1)
                wait(v, "wsmax_s", T // 2 * (b + 1))
                v.tensor_scalar(w_sc[:, :], ws_max[:, :], EPS, 1.0 / QMAX, ALU.max, ALU.mult).then_inc(s["wsc_s"], 1)
                wait(v, "wsc_s", b + 1)
                v.reciprocal(w_rq[:, :], w_sc[:, :]).then_inc(s["wrq_s"], 1)
                wait(v, "wrq_s", b + 1)
                for t in range(WV):
                    v.tensor_scalar(w_in[:, t, :], w_in[:, t, :], w_rq[:, t:t + 1], ROUND, ALU.mult, ALU.add).then_inc(s["wqv_s"], 1)

            def first_scaled(b, t):
                wait(v, "mm1", T * b + t + 1)
                if t < 2:
                    wait(v, "a_s", T * b)
                else:
                    wait(v, "a_s", T * b + t - 1)
                v.scalar_tensor_tensor(out=h_buf[:, t % 2, :], in0=h_bank(t)[:, :], scalar=x_sc[:, t:t + 1],
                                       in1=wsc_bc[:, :], op0=ALU.mult, op1=ALU.mult).then_inc(s["h_s"], 1)

            def first_out_head(b):
                wait(v, "wscbc_s", b + 1)
                first_scaled(b, 0)
                first_scaled(b, 1)

            def first_out(b):
                wait(v, "aqT_s", KI * b)
                for t in range(T):
                    wait(v, "silu_s", T * b + t + 1)
                    v.tensor_tensor(a[:, t, :], silu_g[t % 2], h_buf[:, t % 2, I:2 * I], ALU.mult).then_inc(s["a_s"], 1)
                    if t + 2 < T:
                        first_scaled(b, t + 2)

            def second_weight_max(b):
                wait(v, "cT_in_s", 16 * (b + 1))
                v.tensor_reduce(ac[:, :], cT_in, X, ALU.max, apply_absolute_value=True).then_inc(s["ac_s"], 1)
                wait(v, "ac_s", b + 1)
                v.tensor_scalar(ac_c[:, :], ac[:, :], EPS, None, ALU.max).then_inc(s["acc_s"], 1)
                wait(v, "acc_s", b + 1)
                v.reciprocal(ac_r[:, :], ac_c[:, :]).then_inc(s["acr_s"], 1)

            def second_col_max(b):
                for k in range(KI):
                    wait(v, "tB", NB * b + k + 1)
                    v.tensor_reduce(aa[:, k:k + 1], pB[k % 2][:, :], X, ALU.max,
                                    apply_absolute_value=True).then_inc(s["aa_s"], 1)
                wait(v, "aa_s", KI * (b + 1))
                wait(v, "acr_s", b + 1)
                v.scalar_tensor_tensor(out=ratio2[:, :], in0=aa[:, :], scalar=EPS, in1=ac_r[:, :],
                                       op0=ALU.max, op1=ALU.mult).then_inc(s["ratio2_s"], 1)

            def second_smooth(b):
                wait(v, "s2raw_s", b + 1)
                v.tensor_scalar(s2_col[:, :], s2_raw[:, :], EPS, None, ALU.max).then_inc(s["s2col_s"], 1)
                wait(v, "s2col_s", b + 1)
                v.reciprocal(s2_inv[:, :], s2_col[:, :]).then_inc(s["s2inv_s"], 1)

            def second_a_max(b):
                wait(v, "as_s", T * (b + 1))
                v.tensor_reduce(as_max[:, :], a[:, :, :], X, ALU.max, apply_absolute_value=True).then_inc(s["asmax_s"], 1)
                wait(v, "asmax_s", b + 1)
                v.tensor_scalar(a_sc[:, :], as_max[:, :], EPS, 1.0 / QMAX, ALU.max, ALU.mult).then_inc(s["asc_s"], 1)
                wait(v, "asc_s", b + 1)
                v.reciprocal(a_rq[:, :], a_sc[:, :]).then_inc(s["arq_s"], 1)

            def second_a_quant(b):
                wait(v, "arq_s", b + 1)
                for t in range(T):
                    v.tensor_scalar(a[:, t, :], a[:, t, :], a_rq[:, t:t + 1], ROUND, ALU.mult, ALU.add).then_inc(s["aq_s"], 1)

            def second_quant_c(b):
                v.wait_ge(s["crq_s"], b + 1)
                for t in range(T):
                    v.tensor_scalar(c_in[:, t, :], c_in[:, t, :], c_rq[:, t:t + 1], ROUND, ALU.mult, ALU.add).then_inc(s["cq_s"], 1)

            def second_scale_c(b):
                v.wait_ge(s["is2_s"], b + 1)
                v.wait_ge(s["c_in_s"], 16 * (b + 1))
                for t in range(T):
                    v.tensor_tensor(c_in[:, t, :], c_in[:, t, :], is2_bc[:, 1, :], ALU.mult).then_inc(s["cs_s"], 1)

            def second_c_scale(b):
                wait(v, "cs_s", T * (b + 1))
                v.tensor_reduce(cs_max[:, :], c_in, X, ALU.max, apply_absolute_value=True).then_inc(s["csmax_s"], 1)
                wait(v, "csmax_s", b + 1)
                v.tensor_scalar(c_sc[:, :], cs_max[:, :], EPS, 1.0 / QMAX, ALU.max, ALU.mult).then_inc(s["csc_s"], 1)
                wait(v, "csc_s", b + 1)
                v.reciprocal(c_rq[:, :], c_sc[:, :]).then_inc(s["crq_s"], 1)

            def second_out(b, tiles):
                wait(v, "cscbc_s", b + 1)
                for t in tiles:
                    wait(v, "mm2", T * b + t + 1)
                    if t >= 2:
                        wait(v, "res_s", T * b + t - 1)
                    v.scalar_tensor_tensor(out=y_tmp[:, t % 2, :], in0=pY[t % 2][:, :], scalar=a_sc[:, t:t + 1],
                                           in1=csc_bc[:, :], op0=ALU.mult, op1=ALU.mult).then_inc(s["y_s"], 1)

            def second_norm(b):
                for t in range(T):
                    wait(v, "res_s", T * b + t + 1)
                    v.bn_stats(r_st[:, t, :], x_res[:, t, :]).then_inc(s["r_stats"], 1)
                wait(v, "r_stats", T * (b + 1))
                v.memset(spare[:, :], 0.0)
                for t in range(T):
                    v.bn_aggr(r_mv[:, t, :], r_st[:, t, :]).then_inc(s["r_aggr"], 1)
                wait(v, "r_aggr", T * (b + 1))
                v.tensor_scalar(r_var[:, :], r_mv[:, :, 1], EPS_LN, None, ALU.add).then_inc(s["r_var_s"], 1)

            def second_norm_out(b):
                wait(v, "r_rstd_s", b + 1)
                wait(v, "xn2_out_s", 16 * b)
                wait(v, "xn2T_s", T * b)
                for t in range(T):
                    v.tensor_scalar(xn2[:, t, :], x_res[:, t, :], r_mv[:, t, 0:1], r_rstd[:, t:t + 1],
                                    ALU.subtract, ALU.mult).then_inc(s["xn2_s"], 1)

            def second_scores(b):
                wait(v, "router", b + 1)
                v.tensor_copy(scores[:, bass.ds(b * T, T), :],
                              pY[1][:, 0:T * E].rearrange("p (t e) -> p t e", t=T)).then_inc(s["score_s"], 1)

            def both(b, more=True):
                second_c_scale(b - 1)
                first_scale_x(b)
                first_row_scale(b)
                first_weight_scale(b)
                second_out(b - 1, range(2))
                if more:
                    first_stats(b + 1)
                second_out(b - 1, range(2, T))
                second_norm(b - 1)
                first_out_head(b)
                if more:
                    first_norm(b + 1)
                second_norm_out(b - 1)
                first_out(b)
                second_weight_max(b)
                second_col_max(b)
                if more:
                    first_col_max(b + 1, range(2))
                second_smooth(b)
                if more:
                    first_weight_max(b + 1)
                    first_col_max(b + 1, range(2, KD))
                    first_ratio(b + 1)
                if not more:
                    second_scale_c(b)
                    second_c_scale(b)
                    second_quant_c(b)
                second_scores(b - 1)
                second_a_max(b)
                if more:
                    first_smooth(b + 1)
                second_a_quant(b)

            first_stats(0)
            first_norm(0)
            first_weight_max(0)
            first_col_max(0, range(KD))
            first_ratio(0)
            first_smooth(0)
            first_scale_x(0)
            second_weight_max(0)
            first_row_scale(0)
            first_weight_scale(0)
            split_low(0)
            first_stats(1)
            first_out_head(0)
            first_norm(1)
            first_out(0)
            second_col_max(0)
            first_col_max(1, range(2))
            second_smooth(0)
            first_weight_max(1)
            first_col_max(1, range(2, KD))
            first_ratio(1)
            second_a_max(0)
            first_smooth(1)
            second_a_quant(0)
            with v.Fori(1, B - 1) as b:
                both(b)
            both(B - 1, more=False)
            b = B - 1
            split_low(B)
            second_out(b, range(T))
            second_norm(b)
            second_norm_out(b)
            v.wait_ge(s["cqT_s"], KI * B)
            split_low(EARLY)
            second_scores(b)

            v.wait_ge(s["cscbc_s"], B)
            v.memset(h[:, H:HP], 0.0).then_inc(s["h_pad_s"], 1)
            v.wait_ge(s["consts_a"], N_CONST)
            v.wait_ge(s["score_s"], B)
            n_rt = [0]

            def step(instruction):
                n_rt[0] += 1
                instruction.then_inc(s["rt"], 1)
                v.wait_ge(s["rt"], n_rt[0])

            def over_e(ap):
                return ap.rearrange("p (i a) -> p i a", a=1).to_broadcast([P, NTOK, E])

            for k in range(TOPK):
                v.tensor_copy(row_no[:, k, :], row_id[:, :])
            pref_b = pref[:, :].rearrange("p (a e) -> p a e", a=1).to_broadcast([P, NTOK, E])
            for k in range(TOPK):
                src = scores if k == 0 else sc2
                step(v.tensor_reduce(top[:, k, :], src[:, :, :], X, ALU.max))
                step(v.tensor_tensor(tmp_e[:, :, :], src[:, :, :], over_e(top[:, k, :]), ALU.is_equal))
                step(v.tensor_tensor(tmp_e[:, :, :], tmp_e[:, :, :], pref_b, ALU.mult))
                step(v.tensor_reduce(pick[:, k, :], tmp_e[:, :, :], X, ALU.max))
                step(v.tensor_tensor(ohs[:, k, :, :], pref_b, over_e(pick[:, k, :]), ALU.is_equal))
                if k == 0:
                    step(v.scalar_tensor_tensor(out=sc2[:, :, :], in0=ohs[:, 0, :, :], scalar=-BIG, in1=scores[:, :, :],
                                                op0=ALU.mult, op1=ALU.add))
            v.tensor_tensor(used[:, 0:NTOK, :], ohs[:, 0, :, :], ohs[:, 1, :, :], ALU.add).then_inc(s["used_s"], 1)
            step(v.tensor_tensor(gap, top[:, 1, :], top[:, 0, :], ALU.subtract))
            assert n_rt[0] == GAP_STEP
            v.wait_ge(s["prefix"], 1)
            step(v.tensor_scalar(n_tiles[:, :], pH[0][:, NTOK * E:(NTOK + 1) * E], 1.0 / P,
                                 (P - 1.0) / P - 0.5 + 1.0 / 512, ALU.mult, ALU.add))
            step(v.tensor_scalar(n_tiles[:, :], n_tiles[:, :], ROUND, ROUND, ALU.add, ALU.subtract))
            step(v.tensor_tensor_scan(n_ends[:, :], ones_e[:, :], n_tiles[:, :], 0.0, ALU.mult, ALU.add))
            step(v.tensor_tensor(n_starts[:, :], n_ends[:, :], n_tiles[:, :], ALU.subtract))
            starts_b = n_starts[:, :].rearrange("p (a e) -> p a e", a=1).to_broadcast([P, NTOK, E])
            step(v.scalar_tensor_tensor(out=pos_e[:, :, :], in0=starts_b, scalar=float(P),
                                        in1=pH[0][:, 0:NTOK * E].rearrange("p (i e) -> p i e", e=E),
                                        op0=ALU.mult, op1=ALU.add))
            for k in range(TOPK):
                step(v.tensor_tensor(tmp_e[:, :, :], ohs[:, k, :, :], pos_e[:, :, :], ALU.mult))
                step(v.tensor_reduce(pos[:, k, :], tmp_e[:, :, :], X, ALU.add))
            step(v.tensor_scalar(tile_x[:, :, :], pos[:, :, :], 1.0 / P, -0.5 + 1.0 / 512, ALU.mult, ALU.add))
            step(v.tensor_scalar(tile_of[:, :, :], tile_x[:, :, :], ROUND, ROUND, ALU.add, ALU.subtract))
            step(v.scalar_tensor_tensor(out=slot_of[:, :, :], in0=tile_of[:, :, :], scalar=-float(P), in1=pos[:, :, :],
                                        op0=ALU.mult, op1=ALU.add))
            J = TOPK * NTOK
            tile_b = tile_of[:, :, :].rearrange("p k i -> p (k i)").rearrange("p (j a) -> p j a", a=1).to_broadcast([P, J, NT])
            iota_tb = iota_t[:, :].rearrange("p (a t) -> p a t", a=1).to_broadcast([P, J, NT])
            step(v.tensor_tensor(in_tile, iota_tb, tile_b, ALU.is_equal))
            row_b = row_no.rearrange("p k i -> p (k i)").rearrange("p (j a) -> p j a", a=1).to_broadcast([P, J, NT])
            v.tensor_tensor(row_entry, in_tile, row_b, ALU.mult)
            iota_pb = iota_p[:, :].rearrange("p (a m) -> p a m", a=1).to_broadcast([P, NTOK, P])
            v.wait_ge(s["init_s"], 16)
            for k in range(TOPK):
                slot_b = slot_of[:, k, :].rearrange("p (j a) -> p j a", a=1).to_broadcast([P, NTOK, P])
                v.tensor_tensor(in_slot[:, k * NTOK:(k + 1) * NTOK, :], iota_pb, slot_b, ALU.is_equal
                                ).then_inc(s["table_free"], 1)
            ends_b = n_ends[:, :].rearrange("p (a e) -> p a e", a=1).to_broadcast([P, NT, E])
            iota_te = iota_t[:, :].rearrange("p (t a) -> p t a", a=1).to_broadcast([P, NT, E])
            step(v.tensor_tensor(late_t[:, :, :], iota_te, ends_b, ALU.is_ge))
            step(v.tensor_reduce(te_f[:, :], late_t[:, :, :], X, ALU.add))
            v.tensor_scalar(te[:, :], te_f[:, :], float(E - 1), None, ALU.min).then_inc(s["te_s"], 1)
            v.wait_ge(s["table"], 1)
            step(v.tensor_copy(tab[:, 0, :], pH[1][:, 0:NT]))
            step(v.tensor_scalar(unf[:, :], tab[:, 0, :], 0.0, trash_id[:, 0:1], ALU.is_equal, ALU.mult))
            v.tensor_scalar(gather_id, tab[:, 0, :], -1.0, 0.0, ALU.add, ALU.max).then_inc(s["idx_s"], 1)
            v.scalar_tensor_tensor(out=add_id, in0=unf[:, :], scalar=-1.0, in1=tab[:, 0, :],
                                   op0=ALU.add, op1=ALU.add).then_inc(s["idx_s"], 1)
            v.wait_ge(s["exp_s"], 1)
            step(v.tensor_scalar(den, ex, 1.0, None, ALU.add))
            step(v.reciprocal(prob[:, 0, :], den))
            step(v.tensor_tensor(prob[:, 1, :], ex, prob[:, 0, :], ALU.mult))
            step(v.tensor_copy(p_hi[:, :, :], prob[:, :, :]))
            step(v.tensor_tensor(prob_lo, prob[:, :, :], p_hi[:, :, :], ALU.subtract))
            v.wait_ge(s["whi_g"], 4)
            v.scalar_tensor_tensor(out=piece(w_lo, E - 1, 1), in0=w_stage[1][:, :], scalar=WSCALE,
                                   in1=piece(w_hi, E - 1, 1), op0=ALU.mult, op1=ALU.subtract).then_inc(s["wlo_s"], 1)

            def low_x(t):
                v.wait_ge(s["x_hi_s"], t + 1)
                v.tensor_tensor(x_lo[:, :, :].rearrange("p k m -> p (k m)"), pA[0][:, :],
                                x_hi[:, :, :].rearrange("p k m -> p (k m)"), ALU.subtract).then_inc(s["x_lo_s"], 1)

            def tile(t, more=True):
                v.wait_ge(s["gate_s_s"], t + 1)
                wait(v, "pTt", t)
                v.scalar_tensor_tensor(out=h[:, 0:H], in0=pH[1][:, 0:H], scalar=1.0 / WSCALE, in1=gate_s[:, :],
                                       op0=ALU.mult, op1=ALU.mult).then_inc(s["h_ready"], 1)
                if more:
                    low_x(t + 1)
                v.wait_ge(s["h_hi_s"], t + 1)
                v.tensor_tensor(h_lo[:, :, :].rearrange("p k m -> p (k m)"), pB[0][:, 0:HP],
                                h_hi[:, :, :].rearrange("p k m -> p (k m)"), ALU.subtract).then_inc(s["h_lo_s"], 1)

            low_x(0)
            v.wait_ge(s["wlo_g"], low_count(E - 2, 1))
            for n_v, src in enumerate((p_hi[:, :, :], prob_lo)):
                prob_b = src.rearrange("p k i -> p (k i)").rearrange("p (j a) -> p j a", a=1).to_broadcast([P, J, NT])
                last = v.tensor_tensor(prob_entry[:, :, n_v, :], in_tile, prob_b, ALU.mult)
            last.then_inc(s["table_free"], 1)
            tile(0)
            v.wait_ge(s["table"], 2)
            step(v.tensor_copy(tab[:, 1:3, :], pY[1][:, 0:2 * NT].rearrange("p (v t) -> p v t", v=2)))
            step(v.tensor_tensor(slot_w, tab[:, 1, :], tab[:, 2, :], ALU.add))
            v.wait_ge(s["gate_t_s"], 1)
            v.tensor_scalar(slot_w, slot_w, gates_t[:, 1:2], 1.0 / WSCALE, ALU.mult, ALU.mult).then_inc(s["idx_s"], 1)
            with v.Fori(1, NT - 1) as t:
                tile(t)
            tile(NT - 1, more=False)

        @block.scalar
        def _(act):
            def split_high(e):
                for n, (lo, hi) in enumerate(PIECES):
                    act.wait_ge(wl[n], 16 * (e + 1))
                    act.activation(piece(w_hi, e, n), w_stage[n][:, :], ACT.Copy, scale=WSCALE).then_inc(s["whi_s"], 1)

            def split_high_late(e, n):
                if e == E - 2:
                    act.wait_ge(wl_late[n], 16)
                else:
                    act.wait_ge(wl[n], 16 * (EARLY + 2))
                act.activation(piece(w_hi, e, n), stage_of(e)[n], ACT.Copy, scale=WSCALE).then_inc(s["whi_g"], 1)

            def scale(e, n):
                if isinstance(e, int) and e > EARLY:
                    act.wait_ge(s["whi_g"], 2 * (e - EARLY - 1) + n + 1)
                else:
                    act.wait_ge(s["whi_s"], 2 * e + n + 1)
                act.activation(stage_of(e)[n], stage_of(e)[n], ACT.Copy, scale=WSCALE).then_inc(s["w_scaled"], 1)

            def first_broadcast(b):
                wait(act, "tA", NA * b + 5)
                wait(act, "xs_s", (T - XV) * b)
                wait(act, "xsv_s", XV * b)
                act.activation(inv_bc[:, :], pA[0][:, :], ACT.Copy).then_inc(s["invbc_s"], 1)
                wait(act, "tA", NA * b + 6)
                wait(act, "ws_s", T * b)
                act.activation(s_bc[:, :], pA[1][:, :], ACT.Copy).then_inc(s["sbc_s"], 1)

            def first_quant_rows(b):
                wait(act, "mm1", T * b)
                for k in range(KD):
                    wait(act, "tA", NA * b + 7 + k)
                    act.activation(xqT[:, k, :], pA[k % 2][:, :], ACT.Copy, bias=-ROUND).then_inc(s["xqT_s"], 1)

            def first_quant(b):
                wait(act, "wrq_s", b + 1)
                for t in range(WV, T):
                    act.activation(w_in[:, t, :], w_in[:, t, :], ACT.Identity, bias=round_col[:, 0:1],
                                   scale=w_rq[:, t:t + 1]).then_inc(s["wq_s"], 1)
                for k in range(KD):
                    wait(act, "tA", NA * b + 11 + k)
                    act.activation(wqT[:, k, :], pA[k % 2][:, :], ACT.Copy, bias=-ROUND).then_inc(s["wqT_s"], 1)
                wait(act, "tA", NA * b + 15)
                wait(act, "h_s", T * b)
                act.activation(wsc_bc[:, :], pA[0][:, :], ACT.Copy).then_inc(s["wscbc_s"], 1)

            def first_silu(b, tiles):
                for t in tiles:
                    wait(act, "h_s", T * b + t + 1)
                    wait(act, "a_s", T * b + t - 1)
                    act.activation(silu_g[t % 2], h_buf[:, t % 2, 0:I], ACT.Silu).then_inc(s["silu_s"], 1)

            def second_broadcast(b):
                wait(act, "tB", NB * b + 3)
                wait(act, "as_s", T * b)
                wait(act, "cs_s", T * b)
                act.activation(is2_bc[:, :, :].rearrange("p a i -> p (a i)"), pB[0][:, :], ACT.Copy).then_inc(s["is2_s"], 1)

            def second_quant_rows(b):
                wait(act, "mm2", T * b)
                for k in range(KI):
                    wait(act, "tB", NB * b + 4 + k)
                    act.activation(aqT[:, k, :], pB[(3 + k) % 2][:, :], ACT.Copy, bias=-ROUND).then_inc(s["aqT_s"], 1)

            def second_quant_c(b):
                wait(act, "crq_s", b + 1)
                for t in range(T):
                    act.activation(c_in[:, t, :], c_in[:, t, :], ACT.Identity, bias=round_col[:, 0:1],
                                   scale=c_rq[:, t:t + 1]).then_inc(s["cq_s"], 1)

            def second_quant(b):
                for k in range(KI):
                    wait(act, "tB", NB * b + 6 + k)
                    act.activation(cqT[:, k, :], pB[(5 + k) % 2][:, :], ACT.Copy, bias=-ROUND).then_inc(s["cqT_s"], 1)
                wait(act, "tB", NB * b + 8)
                wait(act, "y_s", T * b)
                act.activation(csc_bc[:, :], pB[1][:, :], ACT.Identity, scale=gates_t[:, 0:1]).then_inc(s["cscbc_s"], 1)

            def rows_of(dram, b):
                return dram[bass.ds(b * S, S), :].rearrange("(t p) d -> p t d", p=P)

            def store_residual(b):
                wait(act, "res_s", T * (b + 1))
                act.dma_start(rows_of(rows, b), x_res).then_inc(s["x_out_s"], 16)

            def store_rows(b):
                wait(act, "xn2_s", T * (b + 1))
                act.dma_start(rows_of(xn2_rows, b), xn2).then_inc(s["xn2_out_s"], 16)

            def second_rows(b, tiles):
                for t in tiles:
                    wait(act, "tB", NB * b + 9 + t)
                    wait(act, "logits", b)
                    act.activation(xn2T[:, t, :, :].rearrange("p k m -> p (k m)"), pB[(8 + t) % 2][:, :],
                                   ACT.Copy).then_inc(s["xn2T_s"], 1)

            def second_logits(b):
                wait(act, "logits", b + 1)
                act.activation(logits, pY[0][0:E, :], ACT.Copy).then_inc(s["logits_s"], 1)

            act.wait_ge(s["g_in_s"], 32)
            act.activation(gates_t[:, :], gates[:, :], ACT.Tanh).then_inc(s["gate_t_s"], 1)
            act.wait_ge(s["consts_a"], N_CONST)
            act.wait_ge(s["gate_t_s"], 1)
            first_broadcast(0)
            split_high(0)
            first_quant_rows(0)
            first_quant(0)
            first_silu(0, range(T))
            second_broadcast(0)
            first_broadcast(1)
            second_quant_rows(0)

            def both(b, more=True):
                second_quant_c(b - 1)
                second_quant(b - 1)
                first_quant_rows(b)
                first_quant(b)
                split_high(b)
                store_residual(b - 1)
                first_silu(b, range(2))
                scale(b, 0)
                second_rows(b - 1, range(T))
                first_silu(b, range(2, T))
                scale(b, 1)
                store_rows(b - 1)
                second_broadcast(b)
                second_logits(b - 1)
                if more:
                    first_broadcast(b + 1)
                else:
                    split_high(B)
                second_quant_rows(b)

            with act.Fori(1, B - 1) as b:
                both(b)
            both(B - 1, more=False)
            b = B - 1
            second_quant(b)
            split_high_late(E - 2, 0)
            split_high(EARLY)
            store_residual(b)
            second_rows(b, range(T))
            second_logits(b)
            split_high_late(E - 2, 1)
            scale(E - 2, 0)
            scale(E - 2, 1)

            act.wait_ge(s["used_s"], 1)
            act.wait_ge(s["rt"], GAP_STEP)
            act.activation(ex, gap, ACT.Exp).then_inc(s["exp_s"], 1)
            act.wait_ge(s["x_out_s"], 16 * B)
            split_high_late(E - 1, 0)
            split_high_late(E - 1, 1)
            scale(E - 1, 0)

            def high_x(t):
                act.wait_ge(s["pXt"], t + 1)
                act.activation(x_hi[:, :, :].rearrange("p k m -> p (k m)"), pA[0][:, :], ACT.Copy).then_inc(s["x_hi_s"], 1)

            def gate(t):
                act.wait_ge(s["up"], t + 1)
                wait(act, "h_ready", t)
                act.activation(gate_s[:, :], pH[0][:, 0:H], ACT.Silu, scale=1.0 / WSCALE).then_inc(s["gate_s_s"], 1)

            def high_h(t):
                act.wait_ge(s["pTt"], t + 1)
                act.activation(h_hi[:, :, :].rearrange("p k m -> p (k m)"), pB[0][:, 0:HP], ACT.Copy).then_inc(s["h_hi_s"], 1)

            def weigh(t, j, free):
                act.wait_ge(s["down"], t + 1)
                if free is not None:
                    act.wait_ge(added[j], free)
                act.activation(y_out[:, j, :], pY[0][:, :], ACT.Copy, scale=slot_w[:, bass.ds(t, 1)]).then_inc(s["y_ready"], 1)

            act.wait_ge(s["wlo_g"], low_count(E - 2, 1))
            high_x(0)
            gate(0)
            high_x(1)
            high_h(0)
            act.wait_ge(s["idx_s"], 3)
            turns = NT // XG - 1
            with act.Fori(0, turns) as i:
                for j in range(1, XG + 1):
                    t = i * XG + j
                    gate(t)
                    high_x(t + 1)
                    weigh(t - 1, j - 1, i * 16)
                    high_h(t)
            for t in range(turns * XG + 1, NT):
                gate(t)
                if t + 1 < NT:
                    high_x(t + 1)
                weigh(t - 1, (t - 1) % XG, turns * 16)
                high_h(t)
            weigh(NT - 1, (NT - 1) % XG, turns * 16)

        @block.tensor
        def _(pe):
            def transpose_chunk(out, src, k):
                for t in range(T):
                    last = pe.transpose(out[:, t * P:(t + 1) * P], src[:, t, k * P:(k + 1) * P], ident[:, :])
                return last

            def broadcast_cols(out, cols, n_cols):
                for k in range(n_cols):
                    last = pe.transpose(out[:, k * P:(k + 1) * P], cols[:, k:k + 1].to_broadcast([P, P]), ident[:, :])
                return last

            def first_cols(b, chunks):
                for k in chunks:
                    if k == 0:
                        wait(pe, "xn_s", T * (b + 1))
                    if k == 0:
                        wait(pe, "h_s", T * b)
                    elif k >= 2:
                        wait(pe, "ax_s", KD * b + k - 1)
                    transpose_chunk(pA[k % 2], xn, k).then_inc(s["tA"], 1)

            def first_broadcasts(b):
                wait(pe, "sinv_s", b + 1)
                wait(pe, "ax_s", KD * (b + 1))
                broadcast_cols(pA[0], s_inv, KD).then_inc(s["tA"], 1)
                broadcast_cols(pA[1], s_col, KD).then_inc(s["tA"], 1)

            def first_rows(b):
                wait(pe, "xq_s", T * (b + 1))
                for k in range(KD):
                    if k == 0:
                        wait(pe, "invbc_s", b + 1)
                    elif k == 1:
                        wait(pe, "sbc_s", b + 1)
                    else:
                        wait(pe, "xqT_s", KD * b + k - 1)
                    transpose_chunk(pA[k % 2], xn, k).then_inc(s["tA"], 1)

            def first_weights(b):
                wait(pe, "wqv_s", WV * (b + 1))
                wait(pe, "wq_s", (T - WV) * (b + 1))
                for k in range(KD):
                    if k < 2:
                        wait(pe, "xqT_s", KD * b + 3 + k)
                    else:
                        wait(pe, "wqT_s", KD * b + k - 1)
                    transpose_chunk(pA[k % 2], w_in, k).then_inc(s["tA"], 1)
                wait(pe, "wqT_s", KD * b + 3)
                broadcast_cols(pA[0], w_sc, T).then_inc(s["tA"], 1)

            def first_products(b):
                wait(pe, "wqT_s", KD * (b + 1))
                for t in range(T):
                    if t == T - 1:
                        wait(pe, "wscbc_s", b + 1)
                    for k in range(KD):
                        last = pe.matmul(h_bank(t)[:, :], xqT[:, k, t * P:(t + 1) * P], wqT[:, k, :],
                                         start=(k == 0), stop=(k == KD - 1))
                    last.then_inc(s["mm1"], 1)

            def second_cols(b):
                wait(pe, "a_s", T * (b + 1))
                wait(pe, "xn2T_s", T * b)
                for k in range(KI):
                    transpose_chunk(pB[k % 2], a, k).then_inc(s["tB"], 1)

            def second_broadcasts(b):
                wait(pe, "s2inv_s", b + 1)
                broadcast_cols(pB[0][:, 0:I], s2_inv, KI)
                broadcast_cols(pB[0][:, I:2 * I], s2_col, KI).then_inc(s["tB"], 1)

            def second_turn_rows(b):
                wait(pe, "aq_s", T * (b + 1))
                wait(pe, "aa_s", KI * (b + 1))
                transpose_chunk(pB[1], a, 0).then_inc(s["tB"], 1)
                wait(pe, "is2_s", b + 1)
                transpose_chunk(pB[0], a, 1).then_inc(s["tB"], 1)

            def second_turns(b):
                wait(pe, "cq_s", T * (b + 1))
                wait(pe, "aqT_s", KI * b + 1)
                transpose_chunk(pB[1], c_in, 0).then_inc(s["tB"], 1)
                wait(pe, "aqT_s", KI * b + 2)
                transpose_chunk(pB[0], c_in, 1).then_inc(s["tB"], 1)
                wait(pe, "cqT_s", KI * b + 1)
                broadcast_cols(pB[1], c_sc, T).then_inc(s["tB"], 1)

            def second_products(b):
                wait(pe, "cqT_s", KI * (b + 1))
                for t in range(T):
                    if t == 0:
                        wait(pe, "logits_s", b)
                    elif t == 1:
                        wait(pe, "score_s", b)
                    else:
                        wait(pe, "y_s", T * b + t - 1)
                    for k in range(KI):
                        last = pe.matmul(pY[t % 2][:, :], aqT[:, k, t * P:(t + 1) * P], cqT[:, k, :],
                                         start=(k == 0), stop=(k == KI - 1))
                    last.then_inc(s["mm2"], 1)

            def router_turn(b, t):
                wait(pe, "xn2_s", T * b + t + 1)
                if t == 0:
                    wait(pe, "cqT_s", KI * (b + 1))
                elif t == 1:
                    wait(pe, "cscbc_s", b + 1)
                else:
                    wait(pe, "xn2T_s", T * b + t - 1)
                for k in range(KD):
                    last = pe.transpose(pB[(8 + t) % 2][:, k * P:(k + 1) * P], xn2[:, t, k * P:(k + 1) * P], ident[:, :])
                last.then_inc(s["tB"], 1)

            def router_product(b, t):
                wait(pe, "xn2T_s", T * b + t + 1)
                for k in range(KD):
                    last = pe.matmul(pY[0][0:E, t * P:(t + 1) * P], wgT[:, k, :], xn2T[:, t, k, :],
                                     start=(k == 0), stop=(k == KD - 1))
                if t == T - 1:
                    last.then_inc(s["logits"], 1)

            def second_scores(b):
                if isinstance(b, int):
                    wait(pe, "logits_s", b + 1)
                for t in range(T):
                    last = pe.transpose(pY[1][:, t * E:(t + 1) * E], logits[:, t * P:(t + 1) * P], ident[0:E, 0:E])
                last.then_inc(s["router"], 1)

            pe.wait_ge(s["consts_a"], N_CONST)
            first_cols(0, range(KD))
            first_broadcasts(0)
            first_rows(0)
            first_weights(0)
            first_products(0)
            second_cols(0)
            first_cols(1, range(2))
            second_broadcasts(0)
            first_cols(1, range(2, KD))
            first_broadcasts(1)
            second_turn_rows(0)
            pe.wait_ge(s["wg_in_s"], 16)

            def both(b, more=True):
                second_turns(b - 1)
                first_rows(b)
                second_products(b - 1)
                first_weights(b)
                first_products(b)
                for t in range(T):
                    router_turn(b - 1, t)
                second_cols(b)
                if more:
                    first_cols(b + 1, range(2))
                router_product(b - 1, 0)
                if more:
                    router_product(b - 1, 1)
                second_broadcasts(b)
                if not more:
                    router_product(b - 1, 1)
                router_product(b - 1, 2)
                router_product(b - 1, 3)
                if more:
                    first_cols(b + 1, range(2, KD - 1))
                    wait(pe, "logits_s", b)
                    first_cols(b + 1, range(KD - 1, KD))
                second_scores(b - 1)
                if more:
                    first_broadcasts(b + 1)
                second_turn_rows(b)

            with pe.Fori(1, B - 1) as b:
                both(b)
            both(B - 1, more=False)
            b = B - 1
            second_turns(b)
            second_products(b)
            router_turn(b, 0)
            for t in range(1, T):
                router_turn(b, t)
                router_product(b, t - 1)
            router_product(b, T - 1)
            second_scores(b)

            pe.wait_ge(s["used_s"], 1)
            used_all = used[:, :, :].rearrange("p i e -> p (i e)")
            pe.matmul(pH[0][:, 0:(NTOK + 1) * E], before[:, :], used_all, start=True, stop=False)
            for i in range(NTOK):
                last = pe.matmul(pH[0][:, (i + 1) * E:(NTOK + 1) * E], ones[:, :],
                                 used[:, i:i + 1, :].to_broadcast([P, NTOK - i, E]), start=False, stop=(i == NTOK - 1))
            last.then_inc(s["prefix"], 1)
            for j in range(TOPK * NTOK):
                if j % NTOK == 0:
                    pe.wait_ge(s["table_free"], j // NTOK + 1)
                last = pe.matmul(pH[1][:, 0:NT], in_slot[:, j, :], row_entry[:, j, :],
                                 start=(j == 0), stop=(j == TOPK * NTOK - 1))
            last.then_inc(s["table"], 1)

            def turn_x(t, j, count):
                pe.wait_ge(gathered[j], count)
                wait(pe, "x_lo_s", t)
                for k in range(KD):
                    last = pe.transpose(pA[0][:, k * P:(k + 1) * P], xg[:, j, k * P:(k + 1) * P], ident[:, :])
                last.then_inc(s["pXt"], 1)

            def weights(half, e, lo, hi):
                return half[:, bass.ds(e, 1), lo:hi].rearrange("p a n -> p (a n)")

            def up(t, e):
                pe.wait_ge(s["x_lo_s"], t + 1)
                wait(pe, "h_ready", t)
                for part in range(2):
                    for k in range(KD):
                        lo = k * 2 * H + part * H
                        for m, (xs, ws) in enumerate(((x_hi, w_hi), (x_hi, w_lo), (x_lo, w_hi))):
                            last = pe.matmul(pH[part][:, 0:H], xs[:, k, :], weights(ws, e, lo, lo + H),
                                             start=(k == 0 and m == 0), stop=(k == KD - 1 and m == 2))
                last.then_inc(s["up"], 1)

            def turn_h(t):
                pe.wait_ge(s["h_ready"], t + 1)
                wait(pe, "h_lo_s", t)
                for k in range(KH):
                    last = pe.transpose(pB[0][:, k * P:(k + 1) * P], h[:, k * P:(k + 1) * P], ident[:, :])
                last.then_inc(s["pTt"], 1)

            def down(t, e):
                pe.wait_ge(s["h_lo_s"], t + 1)
                wait(pe, "y_ready", t)
                for k in range(KH):
                    lo = WU + k * D
                    for m, (hs, ws) in enumerate(((h_hi, w_hi), (h_hi, w_lo), (h_lo, w_hi))):
                        last = pe.matmul(pY[0][:, :], hs[:, k, :], weights(ws, e, lo, lo + D),
                                         start=(k == 0 and m == 0), stop=(k == KH - 1 and m == 2))
                last.then_inc(s["down"], 1)

            def expert(t):
                return pe.value_load(te[0:1, bass.ds(t, 1)], min_val=0, max_val=E - 1)

            turn_x(0, 0, 16)
            pe.wait_ge(s["wlo_s"], low_count(EARLY, 1) + 1)
            pe.wait_ge(s["wlo_g"], low_count(E - 1, 0))
            pe.wait_ge(s["te_s"], 1)
            pe.wait_ge(s["h_pad_s"], 1)
            pe.wait_ge(s["idx_s"], 1)
            up(0, expert(0))
            pe.wait_ge(s["table_free"], TOPK + 1)
            for j in range(TOPK * NTOK):
                last = pe.matmul(pY[1][:, 0:2 * NT], in_slot[:, j, :], prob_entry[:, j, :, :].rearrange("p v t -> p (v t)"),
                                 start=(j == 0), stop=(j == TOPK * NTOK - 1))
            last.then_inc(s["table"], 1)
            turn_x(1, 1, 16)
            turn_h(0)
            turns = NT // XG - 1
            with pe.Fori(0, turns) as i:
                for j in range(1, XG + 1):
                    t = i * XG + j
                    up(t, expert(t))
                    turn_x(t + 1, (j + 1) % XG, (i + (j + 1) // XG + 1) * 16)
                    down(t - 1, expert(t - 1))
                    turn_h(t)
            for t in range(turns * XG + 1, NT):
                up(t, expert(t))
                if t + 1 < NT:
                    turn_x(t + 1, (t + 1) % XG, ((t + 1) // XG + 1) * 16)
                down(t - 1, expert(t - 1))
                turn_h(t)
            down(NT - 1, expert(NT - 1))


def kernel(x, fside_BxS2xS2_0, ctx_1024, g_xattn, g_ffn, L0_ffn_Wg, L0_ffn_W1, L0_ffn_W2, L0_ffn_W3):
    import numpy as np
    import concourse.bacc as bacc
    from concourse.bass_utils import run_bass_kernel_spmd

    def tiles(m):
        m = np.asarray(m)
        return np.ascontiguousarray(m.reshape(m.shape[0], m.shape[1] // P, P, m.shape[2]).transpose(0, 2, 1, 3))

    def turned(m):
        return tiles(np.asarray(m).transpose(0, 2, 1))

    w3 = np.zeros((E, HP, D), np.float32)
    w3[:, :H, :] = np.asarray(L0_ffn_W3).transpose(0, 2, 1)
    up = np.concatenate([np.asarray(L0_ffn_W1), np.asarray(L0_ffn_W2)], axis=1)
    wexp = np.concatenate([turned(up).reshape(E, P, WU), tiles(w3).reshape(E, P, KH * D)], axis=2)
    arrays = {
        "x_t": tiles(x),
        "w_t": tiles(fside_BxS2xS2_0), "w_turned": turned(fside_BxS2xS2_0),
        "c_t": tiles(ctx_1024), "c_turned": turned(ctx_1024),
        "g_x": np.asarray(g_xattn).reshape(1, 1), "g_f": np.asarray(g_ffn).reshape(1, 1),
        "wg_t": turned(np.asarray(L0_ffn_Wg)[None])[0],
        "wexp": np.ascontiguousarray(wexp),
    }
    nc = bacc.Bacc("TRN2", target_bir_lowering=False, num_devices=1)
    aps = [nc.dram_tensor(k, v.shape, mybir.dt.from_np(v.dtype), kind="ExternalInput").ap() for k, v in arrays.items()]
    rows = nc.dram_tensor("rows", (ROWS + P, D), F32, kind="ExternalOutput").ap()
    xn2_rows = nc.dram_tensor("xn2_rows", (ROWS, D), F32).ap()
    build_program(nc, *aps, rows, xn2_rows)
    r = run_bass_kernel_spmd(nc, [arrays], core_ids=[0])
    return r.results[0]["rows"][:ROWS].reshape(B, S, D)
```
